# Optimizing a Trainium2 kernel written in Bass

```python
import numpy as np
import jax
import jax.numpy as jnp

def _softmax(x, axis=-1):
    return jax.nn.softmax(x, axis=axis)

def _gelu(x):
    return jax.nn.gelu(x, approximate=True)

def _silu(x):
    return jax.nn.silu(x)

def _sigmoid(x):
    return jax.nn.sigmoid(x)

def _layernorm(x, axis=-1, eps=1e-05):
    m = jnp.mean(x, axis=axis, keepdims=True)
    v = jnp.var(x, axis=axis, keepdims=True)
    return (x - m) / jnp.sqrt(v + eps)

def _scatter_add(tgt, idx, src, axis=0):
    return tgt.at[idx].add(src)

def _segment_sum(src, seg, n):
    return jax.ops.segment_sum(src, seg, n)
kernel_name = 'mk_adj_preln_d2_adj_r2_505a44'

def setup_inputs(seed: int=0):
    np.random.seed(seed)
    _w = jnp.asarray

    def _rec_inputs():
        import jax
        import jax.numpy as jnp
        _gk = jax.random.key(seed)
        x = -0.0002928 + 1 * jax.random.normal(jax.random.fold_in(_gk, 1), (4096, 256), jnp.float32)
        _a = jax.random.bernoulli(jax.random.fold_in(_gk, 2), 0.000976562, (4096, 4096))
        _af = _a.astype(jnp.float32)
        adj = _af
        return (x, adj)
    x, adj = _rec_inputs()

    def _L0_gnn_setup():
        import jax, jax.numpy as jnp
        import numpy as np
        N = 4096
        D_IN = 256
        D_OUT = 256
        NEG_BIG = -9000000000000000.0
        key = jax.random.key(seed)
        kx, ka, kw, kb, kn, ke = jax.random.split(key, 6)
        x = jax.random.normal(kx, (N, D_IN), dtype=jnp.float32)
        adj = (jax.random.uniform(ka, (N, N)) > 0.9).astype(jnp.float32)
        stdv = 1.0 / np.sqrt(D_OUT)
        weight = jax.random.uniform(kw, (D_IN, D_OUT), minval=-stdv, maxval=stdv, dtype=jnp.float32)
        bias = jax.random.uniform(kb, (D_OUT,), minval=-stdv, maxval=stdv, dtype=jnp.float32)
        node_w = jax.random.uniform(kn, (D_IN, 1), minval=-1.0, maxval=1.0, dtype=jnp.float32)
        stdv_e = 1.0 / np.sqrt(D_IN)
        edge_w = jax.random.uniform(ke, (D_IN, D_IN), minval=-stdv_e, maxval=stdv_e, dtype=jnp.float32)
        return {'x': x, 'adj': adj, 'weight': weight, 'bias': bias, 'node_w': node_w, 'edge_w': edge_w}
    _L0_gnn_all = _L0_gnn_setup()
    _L0_gnn_in = {k: v for k, v in _L0_gnn_all.items() if k in ('weight', 'bias', 'node_w', 'edge_w')}
    del _L0_gnn_all

    def _L1_gnn_setup():
        import jax, jax.numpy as jnp
        import numpy as np
        KAPPA = -1.0
        EPS = 1e-10
        N, D_IN, D_OUT = (4096, 256, 256)

        def _artan_k(x):
            sc = np.sqrt(-KAPPA)
            return jnp.arctanh(jnp.clip(sc * x, -1.0 + 1e-07, 1.0 - 1e-07)) / sc

        def _tan_k(x):
            sc = np.sqrt(-KAPPA)
            return jnp.tanh(sc * x) / sc

        def _clamp_abs(x, eps=EPS):
            return jnp.where(x >= 0, 1.0, -1.0) * jnp.maximum(jnp.abs(x), eps)

        def _norm(x):
            return jnp.sqrt(jnp.maximum(jnp.sum(x * x, axis=-1, keepdims=True), EPS * EPS))

        def mobius_matvec(W, x):
            x_norm = _norm(x)
            mx = x @ W
            mx_norm = _norm(mx)
            res = _tan_k(mx_norm / x_norm * _artan_k(x_norm)) * (mx / mx_norm)
            return jnp.where(mx_norm <= EPS, 0.0, res)

        def mobius_scalar_mul(r, x):
            x_norm = _norm(x)
            return _tan_k(r * _artan_k(x_norm)) * (x / x_norm)

        def weighted_midpoint_lincomb(A, X):
            gamma = jnp.maximum(2.0 / (1.0 + KAPPA * jnp.sum(X * X, axis=-1, keepdims=True)), 1e-15)
            denom = _clamp_abs(A @ (gamma - 1.0))
            nom = A @ (gamma * X)
            two_mean = nom / denom
            sq = jnp.sum(two_mean * two_mean, axis=-1, keepdims=True)
            a_mean = two_mean / (1.0 + jnp.sqrt(jnp.maximum(1.0 + KAPPA * sq, EPS)))
            alpha = jnp.sum(A, axis=-1, keepdims=True)
            return mobius_scalar_mul(alpha, a_mean)

        def logmap0(x):
            xn = _norm(x)
            return _artan_k(xn) * x / xn

        def expmap0(u):
            un = _norm(u)
            return _tan_k(un) * u / un
        key = jax.random.key(seed)
        k1, k2, k3 = jax.random.split(key, 3)
        X = jax.random.normal(k1, (N, D_IN), dtype=jnp.float32) * 0.001
        A_hat = jax.random.uniform(k2, (N, N), dtype=jnp.float32) / N
        W = jax.random.normal(k3, (D_IN, D_OUT), dtype=jnp.float32) * 0.01
        return {'X': X, 'A_hat': A_hat, 'W': W}
    _L1_gnn_all = _L1_gnn_setup()
    _L1_gnn_in = {k: v for k, v in _L1_gnn_all.items() if k in ('W',)}
    del _L1_gnn_all
    return {'x': x, 'adj': adj, 'L0_gnn_weight': _L0_gnn_in['weight'], 'L0_gnn_bias': _L0_gnn_in['bias'], 'L0_gnn_node_w': _L0_gnn_in['node_w'], 'L0_gnn_edge_w': _L0_gnn_in['edge_w'], 'L1_gnn_W': _L1_gnn_in['W']}

def reference(x, adj, L0_gnn_weight, L0_gnn_bias, L0_gnn_node_w, L0_gnn_edge_w, L1_gnn_W):
    import jax
    import jax.numpy as jnp

    def _L0_gnn_ref(x, adj, weight, bias, node_w, edge_w):
        import jax, jax.numpy as jnp
        import numpy as np
        N = 4096
        D_IN = 256
        D_OUT = 256
        NEG_BIG = -9000000000000000.0
        node_att = jax.nn.softmax(x @ node_w, axis=0)
        h = x @ edge_w
        e = h @ h.T
        e = jnp.where(adj > 0, e, NEG_BIG)
        edge_att = jax.nn.softmax(e, axis=1)
        combined_att = node_att * edge_att
        support = x @ weight
        output = adj * combined_att @ support
        return output + bias

    def _L1_gnn_ref(X, A_hat, W):
        import jax, jax.numpy as jnp
        import numpy as np
        KAPPA = -1.0
        EPS = 1e-10
        N, D_IN, D_OUT = (4096, 256, 256)

        def _artan_k(x):
            sc = np.sqrt(-KAPPA)
            return jnp.arctanh(jnp.clip(sc * x, -1.0 + 1e-07, 1.0 - 1e-07)) / sc

        def _tan_k(x):
            sc = np.sqrt(-KAPPA)
            return jnp.tanh(sc * x) / sc

        def _clamp_abs(x, eps=EPS):
            return jnp.where(x >= 0, 1.0, -1.0) * jnp.maximum(jnp.abs(x), eps)

        def _norm(x):
            return jnp.sqrt(jnp.maximum(jnp.sum(x * x, axis=-1, keepdims=True), EPS * EPS))

        def mobius_matvec(W, x):
            x_norm = _norm(x)
            mx = x @ W
            mx_norm = _norm(mx)
            res = _tan_k(mx_norm / x_norm * _artan_k(x_norm)) * (mx / mx_norm)
            return jnp.where(mx_norm <= EPS, 0.0, res)

        def mobius_scalar_mul(r, x):
            x_norm = _norm(x)
            return _tan_k(r * _artan_k(x_norm)) * (x / x_norm)

        def weighted_midpoint_lincomb(A, X):
            gamma = jnp.maximum(2.0 / (1.0 + KAPPA * jnp.sum(X * X, axis=-1, keepdims=True)), 1e-15)
            denom = _clamp_abs(A @ (gamma - 1.0))
            nom = A @ (gamma * X)
            two_mean = nom / denom
            sq = jnp.sum(two_mean * two_mean, axis=-1, keepdims=True)
            a_mean = two_mean / (1.0 + jnp.sqrt(jnp.maximum(1.0 + KAPPA * sq, EPS)))
            alpha = jnp.sum(A, axis=-1, keepdims=True)
            return mobius_scalar_mul(alpha, a_mean)

        def logmap0(x):
            xn = _norm(x)
            return _artan_k(xn) * x / xn

        def expmap0(u):
            un = _norm(u)
            return _tan_k(un) * u / un
        XW = mobius_matvec(W, X)
        AXW = weighted_midpoint_lincomb(A_hat, XW)
        return expmap0(jax.nn.relu(logmap0(AXW)))
    h = jnp.maximum(_layernorm(x, axis=-1), 0.0)
    x = x + _L0_gnn_ref(h, adj, L0_gnn_weight, L0_gnn_bias, L0_gnn_node_w, L0_gnn_edge_w)
    h = jnp.maximum(_layernorm(x, axis=-1), 0.0)
    x = x + _L1_gnn_ref(h, adj, L1_gnn_W)
    return x

_drawn_inputs = setup_inputs


def setup_inputs(seed=0):
    import zlib

    import numpy as np

    out = dict(_drawn_inputs(seed))
    spreads = {}
    factors = {'L0_gnn_weight': 8.0, 'L0_gnn_node_w': 8.0, 'L0_gnn_edge_w': 8.0}
    for name, (base, spread) in spreads.items():
        noise = np.random.default_rng([zlib.crc32(name.encode()), seed]).standard_normal(out[name].shape)
        drawn = base * np.exp(spread * noise) if base else spread * noise
        out[name] = jnp.asarray(drawn.astype(out[name].dtype))
    for name, factor in factors.items():
        out[name] = (out[name] * factor).astype(out[name].dtype)
    return out
```

```python
from contextlib import ExitStack

import concourse.bass as bass
from concourse import mybir

P = 128
ALU = mybir.AluOpType
ACT = mybir.ActivationFunctionType
F32 = mybir.dt.float32
BF16 = mybir.dt.bfloat16
I32 = mybir.dt.int32
AX = mybir.AxisListType.X
RMAX = bass.bass_isa.ReduceOp.max
RADD = bass.bass_isa.ReduceOp.add

LN_EPS = 1e-5
EPS = 1e-10
CLIP = 1.0 - 1e-7
NEG_BIG = -9000000000000000.0
GB = 4


def gnn_program(nc, x, adj, weight, bias, node_w, edge_w, W1, out):
    N, D = x.shape
    NB = N // P
    NG = NB // GB
    KD = D // P
    DY = D + 1
    DYP = DY + 3
    CH = 512
    NCH = N // CH
    TPC = CH // P

    table_h = nc.dram_tensor("table_h", [N, D], F32, kind="Internal").ap()
    table_y = nc.dram_tensor("table_y", [N, DYP], F32, kind="Internal").ap()

    rows = lambda t: t.rearrange("(b p) d -> p b d", p=P)
    x_r, out_r, th_r, ty_r = rows(x), rows(out), rows(table_h), rows(table_y)

    with ExitStack() as ctx:
        def sb(name, shape, dt=F32):
            return ctx.enter_context(nc.sbuf_tensor(name, shape, dt))

        def sem(name):
            return ctx.enter_context(nc.semaphore(name))

        bank = [ctx.enter_context(nc.psum_tensor(f"bank{i}", [P, CH], F32)) for i in range(8)]

        ident = sb("ident", [P, P])
        rhs_g = sb("rhs_g", [P, KD, DY])
        w0 = sb("w0", [P, KD, D])
        w1 = sb("w1", [P, KD, D])
        bias_bc = sb("bias_bc", [P, D])
        eps_t = sb("eps_t", [P, 1])
        GXW = 3 * D // 2
        gx = sb("gx", [P, NB, GXW])
        gx_b = gx[:, :, :].rearrange("p b c -> p (b c)").bitcast(BF16).rearrange("p (b c) -> p b c", b=NB)
        x1 = gx[:, :, 0:D]
        logit = sb("logit", [P, NB])
        natt = sb("natt", [P, NB])
        alpha = sb("alpha", [P, NB])
        col = sb("col", [P, 24, NB])
        cs = lambda k: col[:, k, :]
        xs = sb("xs", [P, 2, GB, D])
        hs = sb("hs", [P, 2, GB, D])
        hT = sb("hT", [P, 2, GB, KD, P])
        stats = sb("stats", [P, GB, 6])
        mv = sb("mv", [P, GB, 2])
        std = sb("std", [P, GB])
        rstd = sb("rstd", [P, GB])
        nmr = sb("nmr", [P, GB])
        work = sb("work", [P, 28000])

        def arena(off, *shape, dt=F32):
            n = 1
            for s in shape:
                n *= s
            words = n if dt == F32 else (n + 1) // 2
            v = work[:, off:off + words]
            if dt != F32:
                v = v.bitcast(dt)
            if len(shape) == 2:
                v = v.rearrange("p (a b) -> p a b", a=shape[0])
            if len(shape) == 3:
                v = v.rearrange("p (a b c) -> p a b c", a=shape[0], b=shape[1])
            return v, off + words

        bar = sem("bar")
        bars = {}

        def barrier(eng):
            n = bars.get(eng, 0) + 1
            bars[eng] = n
            eng.drain().then_inc(bar, 1)
            eng.wait_ge(bar, 5 * n)

        def skewed(eng, a, b, b_first=False):
            a(0, 0)
            with eng.Fori(0, NG // 2 - 1) as j:
                for k in (0, 1):
                    g = 2 * j + k
                    if b_first:
                        b(g, k)
                        a(g + 1, 1 - k)
                    else:
                        a(g + 1, 1 - k)
                        b(g, k)
            if b_first:
                b(NG - 2, 0)
                a(NG - 1, 1)
            else:
                a(NG - 1, 1)
                b(NG - 2, 0)
            b(NG - 1, 1)

        grp = lambda g: bass.ds(g * GB, GB) if not isinstance(g, int) else slice(g * GB, g * GB + GB)
        at = lambda b, n=1: bass.ds(b, n) if not isinstance(b, int) else slice(b, b + n)

        class Front:
            def __init__(self, t):
                self.x_in = [sem(f"{t}_x_in0"), sem(f"{t}_x_in1")]
                self.x_used = sem(f"{t}_x_used")
                self.var = sem(f"{t}_var")
                self.sqrt = sem(f"{t}_sqrt")
                self.rstd = sem(f"{t}_rstd")
                self.h = sem(f"{t}_h")
                self.t = sem(f"{t}_t")
                self.hT = sem(f"{t}_hT")
                self.prod = sem(f"{t}_prod")
                self.prod_used = sem(f"{t}_prod_used")

        f0 = Front("f0")
        f1 = Front("f1")

        def front_stats(d, f, src, g):
            for b in range(GB):
                d.bn_stats(stats[:, b, :], src[:, b, :])
            d.drain()
            for b in range(GB):
                d.bn_aggr(mv[:, b, :], stats[:, b, :])
            d.drain().then_inc(f.var, 1)
            d.wait_ge(f.sqrt, g + 1)
            d.reciprocal(rstd[:, :], std[:, :])
            d.drain()
            d.scalar_tensor_tensor(nmr[:, :], mv[:, :, 0], -1.0, rstd[:, :], ALU.mult, ALU.mult)
            d.drain().then_inc(f.rstd, 1)

        def front_norm(a, f, src, g, k):
            a.wait_ge(f.var, g + 1)
            a.activation(std[:, :], mv[:, :, 1], ACT.Sqrt, bias=eps_t[:, 0:1])
            a.drain().then_inc(f.sqrt, 1)
            a.wait_ge(f.rstd, g + 1)
            a.wait_ge(f.t, GB * (g + 1))
            for b in range(GB):
                a.activation(hs[:, k, b, :], src[:, b, :], ACT.Relu, bias=nmr[:, b:b + 1],
                             scale=rstd[:, b:b + 1]).then_inc(f.h, 1)

        def front_transpose(t, f, g, k):
            t.wait_ge(f.hT, g + 1)
            for b in range(GB):
                t.wait_ge(f.h, GB * g + b + 1)
                for c in range(KD):
                    last = t.transpose(bank[b // 2][:, ((b % 2) * KD + c) * P:((b % 2) * KD + c + 1) * P],
                                       hs[:, k, b, c * P:(c + 1) * P], ident[:, :])
                last.then_inc(f.t, 1)

        def front_hT(d, f, g, k):
            d.wait_ge(f.prod, GB * (g + 1))
            for j in range(GB // 2):
                d.wait_ge(f.t, GB * (g + 2) + 2 * j + 2)
                d.tensor_copy(hT[:, k, 2 * j:2 * j + 2, :, :].rearrange("p b c n -> p (b c n)"), bank[j][:, :])
            d.drain().then_inc(f.hT, 1)

        def front_product(t, f, rhs, n, g, k):
            t.wait_ge(f.hT, g + 2)
            t.wait_ge(f.prod_used, g + 1)
            for b in range(GB):
                for c in range(KD):
                    last = t.matmul(bank[2 + b][:, 0:n], hT[:, k, b, c, :], rhs[:, c, 0:n],
                                    start=(c == 0), stop=(c == KD - 1))
                last.then_inc(f.prod, 1)

        ew, o = arena(0, KD, D)
        ewT, o = arena(o, KD, D)
        res, o = arena(o, 2, GB, D)
        nw, o = arena(o, KD)

        s_w = sem("s_w")
        s_ident = sem("s_ident")
        s_ewT = sem("s_ewT")
        s_ewTc = sem("s_ewTc")
        s_eet = sem("s_eet")
        s_hi = sem("s_hi")
        s_rest = sem("s_rest")
        s_restfree = sem("s_restfree")
        s_th = sem("s_th")
        s_red = sem("s_red")
        s_all = sem("s_all")
        s_stored = sem("s_stored")
        s_exp = sem("s_exp")
        s_negmax = sem("s_negmax")

        hn, o = arena(0, NB, D)
        hnT, o = arena(o, KD, N)
        em, o = arena(o, N)
        ad, o = arena(o, N)
        pt, o = arena(o, 2, CH)
        stg, o = arena(o, D)
        gf, o = arena(o, D)
        gT, o = arena(o, KD, P)
        xr, o = arena(o, D)
        ag, o = arena(o, D)
        agT, o = arena(o, KD, P)
        sc, o = arena(o, 8)
        assert o <= 28000, o
        A = {n: sem("ga_" + n) for n in (
            "hn", "staged", "stage_free", "setT", "setTc", "adj", "x", "done", "g", "gT", "gTc", "scores",
            "masked", "max", "exp", "weights", "pt", "ptc", "agg", "aggc", "aggT", "aggTc", "proj")}

        def ga_sp(e):
            e.dma_start(hn, th_r).then_inc(A["hn"], 16)
            with e.Fori(0, NB) as i:
                e.wait_ge(A["done"], i + 1)
                e.dma_start(ad, adj[bass.ds(i * P, P), :]).then_inc(A["adj"], 16)
                e.dma_start(xr, x[bass.ds(i * P, P), :]).then_inc(A["x"], 16)
            e.wait_ge(A["done"], NB + 1)

        def ga_dve(d):
            d.sem_inc(A["done"], 1)
            d.sem_inc(A["masked"], 2)
            d.wait_ge(A["hn"], 16)
            with d.Fori(0, NB) as t:
                d.wait_ge(A["stage_free"], t + 1)
                d.tensor_copy(stg, hn[:, bass.ds(t, 1), :])
                d.drain().then_inc(A["staged"], 1)
            with d.Fori(0, NB) as i:
                gb = gx_b[:, bass.ds(i, 1), :]
                d.tensor_tensor(gf, gb[:, :, 0:D], gb[:, :, D:2 * D], ALU.add)
                d.drain()
                d.tensor_tensor(gf, gf, gb[:, :, 2 * D:3 * D], ALU.add)
                d.drain().then_inc(A["g"], 1)
                d.wait_ge(A["adj"], 16 * (i + 1))
                d.tensor_scalar(em, ad, 0.0, NEG_BIG, ALU.is_le, ALU.mult)
                d.drain()
                for c in range(NCH):
                    d.wait_ge(A["scores"], NCH * i + c + 1)
                    d.tensor_tensor(em[:, c * CH:(c + 1) * CH], em[:, c * CH:(c + 1) * CH],
                                    bank[c % 2][:, :], ALU.add).then_inc(A["masked"], 1)
                d.drain()
                d.tensor_reduce(sc[:, 0:1], em, AX, ALU.max)
                d.drain()
                d.tensor_scalar(sc[:, 1:2], sc[:, 0:1], -1.0, None, ALU.mult)
                d.drain().then_inc(A["max"], 1)
                d.wait_ge(A["exp"], i + 1)
                d.tensor_tensor(em, em, ad, ALU.mult)
                d.drain().then_inc(A["weights"], 1)
                d.reciprocal(sc[:, 3:4], sc[:, 2:3])
                d.wait_ge(A["x"], 16 * (i + 1))
                d.tensor_tensor(xr, xr, bias_bc[:, :], ALU.add)
                d.drain()
                d.tensor_tensor(sc[:, 4:5], sc[:, 3:4], natt[:, bass.ds(i, 1)], ALU.mult)
                d.drain()
                d.wait_ge(A["proj"], i + 1)
                d.scalar_tensor_tensor(x1[:, bass.ds(i, 1), :], bank[7][:, 0:D], sc[:, 4:5], xr, ALU.mult, ALU.add)
                d.drain().then_inc(A["done"], 1)

        def ga_pe(t):
            t.sem_inc(A["stage_free"], 1)
            with t.Fori(0, NB) as i:
                t.wait_ge(A["staged"], i + 1)
                t.wait_ge(A["setTc"], i + 1)
                for c in range(KD):
                    last = t.transpose(bank[2][:, c * P:(c + 1) * P], stg[:, c * P:(c + 1) * P], ident[:, :])
                t.drain().then_inc(A["stage_free"], 1)
                t.sem_inc(A["setT"], 1)
            t.wait_ge(A["setTc"], NB + 1)
            with t.Fori(0, NB) as i:
                t.wait_ge(A["g"], i + 1)
                for c in range(KD):
                    last = t.transpose(bank[2][:, c * P:(c + 1) * P], gf[:, c * P:(c + 1) * P], ident[:, :])
                last.then_inc(A["gT"], 1)
                t.wait_ge(A["gTc"], i + 1)
                for c in range(NCH):
                    t.wait_ge(A["masked"], NCH * i + c + 1)
                    for k in range(KD):
                        last = t.matmul(bank[c % 2][:, :], gT[:, k, :], hnT[:, k, c * CH:(c + 1) * CH],
                                        start=(k == 0), stop=(k == KD - 1))
                    last.then_inc(A["scores"], 1)
                t.wait_ge(A["weights"], i + 1)

                def add_chunk(c):
                    t.wait_ge(A["ptc"], NCH * i + c + 1)
                    for q in range(TPC):
                        n = c * TPC + q
                        last = t.matmul(bank[5][:, 0:D], pt[:, c % 2, q * P:(q + 1) * P], hn[:, n, :],
                                        start=(n == 0), stop=(n == NB - 1))
                    return last

                for c in range(NCH):
                    for q in range(TPC):
                        n = c * TPC + q
                        last = t.transpose(bank[3 + c % 2][:, q * P:(q + 1) * P], em[:, n * P:(n + 1) * P],
                                           ident[:, :])
                    last.then_inc(A["pt"], 1)
                    if c:
                        add_chunk(c - 1)
                add_chunk(NCH - 1).then_inc(A["agg"], 1)
                t.wait_ge(A["aggc"], i + 1)
                for k in range(KD):
                    last = t.transpose(bank[6][:, k * P:(k + 1) * P], ag[:, k * P:(k + 1) * P], ident[:, :])
                last.then_inc(A["aggT"], 1)
                t.wait_ge(A["aggTc"], i + 1)
                for k in range(KD):
                    last = t.matmul(bank[7][:, 0:D], agT[:, k, :], w0[:, k, :], start=(k == 0), stop=(k == KD - 1))
                last.then_inc(A["proj"], 1)

        def ga_act(a):
            a.sem_inc(A["setTc"], 1)
            with a.Fori(0, NB) as t:
                a.wait_ge(A["setT"], t + 1)
                for c in range(KD):
                    a.activation(hnT[:, c, bass.ds(t * P, P)], bank[2][:, c * P:(c + 1) * P], ACT.Copy)
                a.drain().then_inc(A["setTc"], 1)
            with a.Fori(0, NB) as i:
                a.wait_ge(A["gT"], i + 1)
                a.activation(gT.rearrange("p a b -> p (a b)"), bank[2][:, 0:D], ACT.Copy).then_inc(A["gTc"], 1)
                a.wait_ge(A["max"], i + 1)
                a.activation(em, em, ACT.Exp, bias=sc[:, 1:2], accum_out=sc[:, 2:3]).then_inc(A["exp"], 1)
                for c in range(NCH):
                    a.wait_ge(A["pt"], NCH * i + c + 1)
                    a.activation(pt[:, c % 2, :], bank[3 + c % 2][:, :], ACT.Copy).then_inc(A["ptc"], 1)
                a.wait_ge(A["agg"], i + 1)
                a.activation(ag, bank[5][:, 0:D], ACT.Copy).then_inc(A["aggc"], 1)
                a.wait_ge(A["aggT"], i + 1)
                a.activation(agT.rearrange("p a b -> p (a b)"), bank[6][:, 0:D], ACT.Copy).then_inc(A["aggTc"], 1)

        mx, o = arena(0, NB, D)
        ys, o = arena(o, 2, GB, DYP)
        assert o <= 28000
        s_mx = sem("s_mx")
        s_sq = sem("s_sq")
        s_ys = sem("s_ys")
        s_gm = sem("s_gm")
        s_tyo = [sem("s_tyo0"), sem("s_tyo1")]
        s_cc = sem("s_cc")
        s_cd = sem("s_cd")

        s_asked = sem("s_asked")
        s_answered = sem("s_answered")
        asked, answered = [0], [0]

        def ask(d):
            asked[0] += 1
            d.drain().then_inc(s_asked, 1)
            d.wait_ge(s_answered, asked[0])

        def answer(a, o_, i_, func):
            answered[0] += 1
            a.wait_ge(s_asked, answered[0])
            a.activation(o_, i_, func)
            a.drain().then_inc(s_answered, 1)

        def then(d, ins):
            d.drain()

        def root(d, i_):
            d.tensor_scalar(i_, i_, EPS * EPS, None, ALU.max)
            ask(d)

        def artanh(d, o_, i_, y, u, t):
            then(d, d.tensor_scalar(y, i_, CLIP, None, ALU.min))
            then(d, d.tensor_scalar(u, y, -1.0, 1.0, ALU.mult, ALU.add))
            then(d, d.reciprocal(t, u))
            then(d, d.scalar_tensor_tensor(y, y, 2.0, t, ALU.mult, ALU.mult))
            d.tensor_scalar(u, y, 1.0, None, ALU.add)
            ask(d)
            then(d, d.tensor_scalar(u, u, 1.0, None, ALU.subtract))
            then(d, d.tensor_scalar(t, u, 0.0, None, ALU.is_equal))
            d.tensor_tensor(u, u, t, ALU.add)
            then(d, d.tensor_tensor(o_, o_, t, ALU.add))
            then(d, d.reciprocal(t, u))
            then(d, d.scalar_tensor_tensor(o_, o_, 0.5, t, ALU.mult, ALU.mult))
            then(d, d.tensor_tensor(o_, o_, y, ALU.mult))

        S1, S2, XN, MN, ATH, Z, TH, R, Q, GAM, GR, GM1, T1, T2, T3 = (cs(k) for k in range(15))

        def mobius_dve(d):
            root(d, S1)
            root(d, S2)
            artanh(d, ATH, XN, T1, T2, T3)
            then(d, d.reciprocal(T1, XN))
            then(d, d.tensor_tensor(T1, T1, MN, ALU.mult))
            d.tensor_tensor(Z, T1, ATH, ALU.mult)
            ask(d)
            then(d, d.reciprocal(T1, MN))
            d.tensor_tensor(R, TH, T1, ALU.mult)
            then(d, d.tensor_scalar(T2, MN, EPS, None, ALU.is_gt))
            then(d, d.tensor_tensor(R, R, T2, ALU.mult))
            then(d, d.tensor_tensor(Q, R, R, ALU.mult))
            then(d, d.tensor_tensor(Q, Q, S2, ALU.mult))
            then(d, d.tensor_scalar(Q, Q, -1.0, 1.0, ALU.mult, ALU.add))
            then(d, d.reciprocal(T1, Q))
            then(d, d.tensor_scalar(GAM, T1, 2.0, 1e-15, ALU.mult, ALU.max))
            d.tensor_tensor(GR, GAM, R, ALU.mult)
            then(d, d.tensor_scalar(GM1, GAM, 1.0, None, ALU.subtract))

        def mobius_act(a):
            answer(a, XN, S1, ACT.Sqrt)
            answer(a, MN, S2, ACT.Sqrt)
            answer(a, ATH, T2, ACT.Ln)
            answer(a, TH, Z, ACT.Tanh)

        yr, o = arena(0, NB, DYP)
        nom, o = arena(o, NB, DY)
        ad2, o = arena(o, N)
        at2, o = arena(o, 2, CH)
        assert o <= 28000, o
        M = {n: sem("gm_" + n) for n in ("y", "adj", "adj_used", "t", "tc", "nom", "nomc", "alpha")}
        fs = sb("fs", [P, 2, D])

        def gm_sp(e):
            e.dma_start(yr, ty_r).then_inc(M["y"], 16)
            with e.Fori(0, NB) as i:
                e.wait_ge(M["t"], NCH * (i + 1))
                e.wait_ge(M["alpha"], i + 1)
                e.dma_start(ad2, adj[bass.ds(i * P, P), :]).then_inc(M["adj"], 16)

        def gm_pe(t):
            t.sem_inc(M["t"], NCH)
            t.wait_ge(M["y"], 16)
            with t.Fori(0, NB) as i:
                t.wait_ge(M["adj"], 16 * (i + 1))
                t.wait_ge(M["nomc"], i + 1)

                def add_chunk(c):
                    t.wait_ge(M["tc"], NCH * i + c + 1)
                    for q in range(TPC):
                        n = c * TPC + q
                        last = t.matmul(bank[5][:, 0:DY], at2[:, c % 2, q * P:(q + 1) * P], yr[:, n, 0:DY],
                                        start=(n == 0), stop=(n == NB - 1))
                    return last

                for c in range(NCH):
                    for q in range(TPC):
                        n = c * TPC + q
                        last = t.transpose(bank[3 + c % 2][:, q * P:(q + 1) * P], ad2[:, n * P:(n + 1) * P],
                                           ident[:, :])
                    last.then_inc(M["t"], 1)
                    if c:
                        add_chunk(c - 1)
                add_chunk(NCH - 1).then_inc(M["nom"], 1)

        def gm_act(a):
            a.sem_inc(M["nomc"], 1)
            with a.Fori(0, NB) as i:
                for c in range(NCH):
                    a.wait_ge(M["t"], NCH * (i + 1) + c + 1)
                    a.activation(at2[:, c % 2, :], bank[3 + c % 2][:, :], ACT.Copy).then_inc(M["tc"], 1)
                a.wait_ge(M["nom"], i + 1)
                a.activation(nom[:, bass.ds(i, 1), :], bank[5][:, 0:DY], ACT.Copy)
                a.activation(fs[:, 0, :], bank[5][:, 0:D], ACT.Square, accum_out=S0[:, bass.ds(i, 1)])
                a.drain().then_inc(M["nomc"], 1)

        def gm_dve(d):
            d.sem_inc(M["alpha"], 1)
            with d.Fori(0, NB) as i:
                d.wait_ge(M["adj"], 16 * (i + 1))
                d.tensor_reduce(alpha[:, bass.ds(i, 1)], ad2, AX, ALU.add).then_inc(M["alpha"], 1)

        S0, DN, RD, S4, WW, NN, TA, SS1, FF, S5, F3, U1, U2, U3, U4 = (cs(k) for k in range(15))
        den = nom[:, :, D]

        def midpoint_dve(d):
            then(d, d.tensor_scalar(U1, den, 0.0, None, ALU.is_ge))
            then(d, d.tensor_scalar(U1, U1, 2.0, -1.0, ALU.mult, ALU.add))
            then(d, d.tensor_tensor(DN, den, U1, ALU.mult))
            then(d, d.scalar_tensor_tensor(DN, DN, EPS, U1, ALU.max, ALU.mult))
            then(d, d.reciprocal(RD, DN))
            then(d, d.tensor_tensor(S4, S0, RD, ALU.mult))
            then(d, d.tensor_tensor(S4, S4, RD, ALU.mult))
            then(d, d.tensor_scalar(U1, S4, -1.0, 1.0, ALU.mult, ALU.add))
            d.tensor_scalar(U1, U1, EPS, None, ALU.max)
            ask(d)
            then(d, d.tensor_scalar(U2, U2, 1.0, None, ALU.add))
            then(d, d.reciprocal(WW, U2))
            then(d, d.tensor_tensor(U4, WW, WW, ALU.mult))
            then(d, d.tensor_tensor(U4, U4, S4, ALU.mult))
            then(d, d.tensor_copy(U1, U4))
            root(d, U1)
            artanh(d, TA, NN, U1, U2, U3)
            d.tensor_tensor(TA, TA, alpha[:, :], ALU.mult)
            ask(d)
            then(d, d.reciprocal(U1, NN))
            then(d, d.tensor_tensor(SS1, TA, U1, ALU.mult))
            then(d, d.tensor_tensor(U4, U4, SS1, ALU.mult))
            then(d, d.tensor_tensor(U4, U4, SS1, ALU.mult))
            root(d, U4)
            artanh(d, TA, NN, U1, U2, U3)
            then(d, d.reciprocal(U1, NN))
            then(d, d.tensor_tensor(FF, TA, U1, ALU.mult))
            then(d, d.tensor_tensor(FF, FF, SS1, ALU.mult))
            then(d, d.tensor_tensor(FF, FF, WW, ALU.mult))
            then(d, d.tensor_tensor(FF, FF, RD, ALU.mult))

        def midpoint_act(a):
            answer(a, U2, U1, ACT.Sqrt)
            answer(a, NN, U1, ACT.Sqrt)
            answer(a, TA, U2, ACT.Ln)
            answer(a, TA, TA, ACT.Tanh)
            answer(a, NN, U4, ACT.Sqrt)
            answer(a, TA, U2, ACT.Ln)

        def expmap_dve(d):
            root(d, S5)
            ask(d)
            then(d, d.reciprocal(U1, NN))
            then(d, d.tensor_tensor(F3, TA, U1, ALU.mult))

        def expmap_act(a):
            answer(a, NN, S5, ACT.Sqrt)
            answer(a, TA, NN, ACT.Tanh)
        s_u = sem("s_u")
        s_us = sem("s_us")
        s_o = sem("s_o")
        s_out = sem("s_out")

        block = ctx.enter_context(nc.Block())

        @block.sync
        def _(e):
            e.dma_start(ew, edge_w.rearrange("(c p) d -> p c d", p=P)).then_inc(s_w, 16)
            e.dma_start(nw, node_w.rearrange("(c p) d -> p (c d)", p=P), allow_slow_non_contiguous=True).then_inc(s_w, 16)
            e.dma_start(w0[:, :, :], weight.rearrange("(c p) d -> p c d", p=P)).then_inc(s_w, 16)
            e.dma_start(w1[:, :, :], W1.rearrange("(c p) d -> p c d", p=P)).then_inc(s_w, 16)
            e.dma_start(bias_bc[:, :], bias.rearrange("(a d) -> a d", a=1).broadcast_to([P, D])).then_inc(s_w, 16)

            def load(g, k):
                e.wait_ge(f0.x_used, g + 1)
                e.dma_start(xs[:, k, :, :], x_r[:, grp(g), :]).then_inc(f0.x_in[k], 16)

            def store(g, k):
                e.wait_ge(f0.h, GB * (g + 1))
                e.dma_start(th_r[:, grp(g), :], hs[:, k, :, :]).then_inc(s_th, 16)
                e.wait_ge(s_th, 16 * (g + 1))
                e.sem_inc(s_stored, 1)
            e.sem_inc(s_stored, 2)
            load(0, 0)
            skewed(e, lambda g, k: load(g + 1, 1 - k) if not isinstance(g, int) or g + 1 < NG else None, store)
            barrier(e)
            ga_sp(e)
            barrier(e)

            def store_y(g, k):
                e.wait_ge(s_ys, g + 1)
                e.dma_start(ty_r[:, grp(g), :], ys[:, k, :, :]).then_inc(s_tyo[k], 16)
            for g in range(NG):
                store_y(g, g % 2)
            for k in (0, 1):
                e.wait_ge(s_tyo[k], 16 * NG // 2)
            barrier(e)
            gm_sp(e)
            barrier(e)
            for g in range(NG):
                e.wait_ge(s_o, GB * (g + 1))
                e.dma_start(out_r[:, grp(g), :], x1[:, grp(g), :]).then_inc(s_out, 16)
            e.wait_ge(s_out, 16 * NG)

        @block.gpsimd
        def _(p):
            p.memset(ident[:, :], 0.0)
            p.memset(eps_t[:, :], LN_EPS)
            p.memset(ys[:, :, :, :], 0.0)
            p.drain()
            p.affine_select(out=ident[:, :], in_=ident[:, :], compare_op=ALU.not_equal, fill=1.0, base=0,
                            pattern=[[-1, P]], channel_multiplier=1)
            p.drain().then_inc(s_ident, 1)

            def split(g, k):
                for b in range(GB):
                    blk = at(g * GB + b)
                    p.wait_ge(s_rest, GB * g + b + 1)
                    p.tensor_copy(gx_b[:, blk, D:2 * D], res[:, k, b, :])
                    p.drain()
                    p.tensor_tensor(gx_b[:, blk, 2 * D:3 * D], res[:, k, b, :], gx_b[:, blk, D:2 * D],
                                    ALU.subtract)
                p.drain().then_inc(s_restfree, 1)
            p.sem_inc(s_restfree, 2)
            with p.Fori(0, NG // 2) as j:
                split(2 * j, 0)
                split(2 * j + 1, 1)
            p.wait_ge(s_red, 1)
            p.partition_all_reduce(cs(1)[:, 0:1], cs(0)[:, 0:1], P, RMAX)
            p.drain().then_inc(s_all, 1)
            p.wait_ge(s_exp, 1)
            p.partition_all_reduce(cs(1)[:, 2:3], cs(0)[:, 2:3], P, RADD)
            p.drain().then_inc(s_all, 1)
            for _ in range(4):
                barrier(p)

        @block.scalar
        def _(a):
            a.sem_inc(f0.x_used, 2)
            a.wait_ge(s_ident, 1)

            def norm(g, k):
                a.wait_ge(f0.var, g + 1)
                a.activation(std[:, :], mv[:, :, 1], ACT.Sqrt, bias=eps_t[:, 0:1])
                a.drain().then_inc(f0.sqrt, 1)
                a.wait_ge(f0.rstd, g + 1)
                a.wait_ge(f0.t, GB * (g + 1))
                a.wait_ge(s_stored, g + 1)
                for b in range(GB):
                    a.activation(hs[:, k, b, :], xs[:, k, b, :], ACT.Relu, bias=nmr[:, b:b + 1],
                                 scale=rstd[:, b:b + 1]).then_inc(f0.h, 1)
                a.drain().then_inc(f0.x_used, 1)

            def hi(g, k):
                for b in range(GB):
                    a.wait_ge(f0.prod, GB * (g + 2) + b + 1)
                    a.activation(gx_b[:, at(g * GB + b), 0:D], bank[2 + b][:, 0:D], ACT.Copy).then_inc(s_hi, 1)
            skewed(a, norm, hi)
            a.wait_ge(s_negmax, 1)
            a.activation(natt[:, :], logit[:, :], ACT.Exp, bias=cs(1)[:, 1:2], accum_out=cs(0)[:, 2:3])
            a.drain().then_inc(s_exp, 1)
            barrier(a)
            ga_act(a)
            barrier(a)

            def norm1(g, k):
                front_norm(a, f1, x1[:, grp(g), :], g, k)
                a.wait_ge(f1.h, GB * (g + 1))
                for b in range(GB):
                    a.activation(fs[:, 0, :], hs[:, k, b, :], ACT.Square, accum_out=S1[:, at(g * GB + b)])
                    a.drain()

            def mx_out(g, k):
                for b in range(GB):
                    a.wait_ge(f1.prod, GB * (g + 2) + b + 1)
                    a.activation(mx[:, at(g * GB + b), :], bank[2 + b][:, 0:D], ACT.Copy)
                    a.activation(fs[:, 1, :], bank[2 + b][:, 0:D], ACT.Square, accum_out=S2[:, at(g * GB + b)])
                    a.drain()
                a.sem_inc(f1.prod_used, 1)
            a.sem_inc(f1.prod_used, 1)
            skewed(a, norm1, mx_out)
            a.drain().then_inc(s_sq, 1)
            mobius_act(a)
            a.wait_ge(s_gm, 1)
            for g in range(NG):
                if g >= 2:
                    a.wait_ge(s_tyo[g % 2], 16 * (g // 2))
                for b in range(GB):
                    n = g * GB + b
                    a.activation(ys[:, g % 2, b, 0:D], mx[:, n, :], ACT.Copy, scale=GR[:, n:n + 1])
                    a.activation(ys[:, g % 2, b, D:DY], GM1[:, n:n + 1], ACT.Copy)
                a.drain().then_inc(s_ys, 1)
            barrier(a)
            gm_act(a)
            barrier(a)
            midpoint_act(a)
            a.wait_ge(s_u, 1)
            for n in range(NB):
                a.activation(nom[:, n, 0:D], nom[:, n, 0:D], ACT.Relu, scale=FF[:, n:n + 1])
                a.drain()
                a.activation(fs[:, 0, :], nom[:, n, 0:D], ACT.Square, accum_out=S5[:, n:n + 1])
            a.drain().then_inc(s_us, 1)
            expmap_act(a)

        @block.tensor
        def _(t):
            for f in (f0, f1):
                t.sem_inc(f.t, 2 * GB)
                t.sem_inc(f.prod, 2 * GB)
            t.wait_ge(s_ident, 1)
            t.wait_ge(s_w, 80)
            for r in range(KD):
                for c in range(KD):
                    last = t.transpose(bank[6][:, (c * KD + r) * P:(c * KD + r + 1) * P],
                                       ew[:, r, c * P:(c + 1) * P], ident[:, :])
            last.then_inc(s_ewT, 1)
            t.wait_ge(s_ewTc, 1)
            for r in range(KD):
                for c in range(KD):
                    last = t.matmul(bank[7][:, r * D:(r + 1) * D], ewT[:, c, r * P:(r + 1) * P], ewT[:, c, :],
                                    start=(c == 0), stop=(c == KD - 1))
            last.then_inc(s_eet, 1)
            t.wait_ge(s_eet, 2)
            skewed(t, lambda g, k: front_transpose(t, f0, g, k),
                   lambda g, k: front_product(t, f0, rhs_g, DY, g, k), b_first=True)
            barrier(t)
            ga_pe(t)
            barrier(t)
            skewed(t, lambda g, k: front_transpose(t, f1, g, k),
                   lambda g, k: front_product(t, f1, w1, D, g, k), b_first=True)
            barrier(t)
            gm_pe(t)
            barrier(t)

        @block.vector
        def _(d):
            d.wait_ge(s_ewT, 1)
            d.tensor_copy(ewT.rearrange("p a b -> p (a b)"), bank[6][:, :])
            d.drain().then_inc(s_ewTc, 1)
            d.wait_ge(s_eet, 1)
            d.tensor_copy(rhs_g[:, :, 0:D], bank[7][:, :].rearrange("p (a b) -> p a b", a=KD))
            d.wait_ge(s_w, 80)
            d.tensor_copy(rhs_g[:, :, D], nw)
            d.drain().then_inc(s_eet, 1)
            for f in (f0, f1):
                d.sem_inc(f.hT, 1)
            d.sem_inc(f0.prod_used, 1)

            def first(g, k):
                d.wait_ge(f0.x_in[k], 8 * (g - k) + 16)
                front_stats(d, f0, xs[:, k, :, :], g)
                front_hT(d, f0, g, k)

            def rest(g, k):
                d.wait_ge(s_restfree, g + 1)
                for b in range(GB):
                    d.wait_ge(s_hi, GB * g + b + 1)
                    d.tensor_tensor(res[:, k, b, :], bank[2 + b][:, 0:D], gx_b[:, at(g * GB + b), 0:D],
                                    ALU.subtract).then_inc(s_rest, 1)
                    d.tensor_copy(logit[:, at(g * GB + b)], bank[2 + b][:, D:DY])
                d.drain().then_inc(f0.prod_used, 1)
            skewed(d, first, rest)
            d.tensor_reduce(cs(0)[:, 0:1], logit[:, :], AX, ALU.max)
            d.drain().then_inc(s_red, 1)
            d.wait_ge(s_all, 1)
            d.tensor_scalar(cs(1)[:, 1:2], cs(1)[:, 0:1], -1.0, None, ALU.mult)
            d.drain().then_inc(s_negmax, 1)
            d.wait_ge(s_all, 2)
            d.reciprocal(cs(1)[:, 3:4], cs(1)[:, 2:3])
            d.drain()
            d.tensor_scalar(natt[:, :], natt[:, :], cs(1)[:, 3:4], None, ALU.mult)
            barrier(d)
            ga_dve(d)
            barrier(d)

            def first1(g, k):
                front_stats(d, f1, x1[:, grp(g), :], g)
                front_hT(d, f1, g, k)
            with d.Fori(0, NG // 2) as j:
                first1(2 * j, 0)
                first1(2 * j + 1, 1)
            d.wait_ge(s_sq, 1)
            mobius_dve(d)
            d.drain().then_inc(s_gm, 1)
            barrier(d)
            gm_dve(d)
            barrier(d)
            midpoint_dve(d)
            d.drain().then_inc(s_u, 1)
            d.wait_ge(s_us, 1)
            expmap_dve(d)
            d.drain()
            for n in range(NB):
                d.scalar_tensor_tensor(x1[:, n, :], nom[:, n, 0:D], F3[:, n:n + 1], x1[:, n, :], ALU.mult,
                                       ALU.add).then_inc(s_o, 1)


_INS = ['x', 'adj', 'L0_gnn_weight', 'L0_gnn_bias', 'L0_gnn_node_w', 'L0_gnn_edge_w', 'L1_gnn_W']


def kernel(**inputs):
    import numpy as np
    import concourse.bacc as bacc
    from concourse.bass_utils import run_bass_kernel_spmd

    nc = bacc.Bacc("TRN2", target_bir_lowering=False, num_devices=1)
    arrays, args = {}, []
    for name in _INS:
        a = np.ascontiguousarray(inputs[name])
        arrays[f"in_{name}"] = a
        args.append(nc.dram_tensor(f"in_{name}", a.shape, mybir.dt.from_np(a.dtype), kind="ExternalInput").ap())
    out = nc.dram_tensor("out_0", inputs['x'].shape, F32, kind="ExternalOutput").ap()
    gnn_program(nc, *args, out)
    return run_bass_kernel_spmd(nc, [arrays], core_ids=[0]).results[0]["out_0"]
```

```python
from contextlib import ExitStack

import concourse.bass as bass
from concourse import mybir

P = 128
ALU = mybir.AluOpType
ACT = mybir.ActivationFunctionType
F32 = mybir.dt.float32
BF16 = mybir.dt.bfloat16
F16 = mybir.dt.float16
I32 = mybir.dt.int32
AX = mybir.AxisListType.X
RMAX = bass.bass_isa.ReduceOp.max
RADD = bass.bass_isa.ReduceOp.add

LN_EPS = 1e-5
EPS = 1e-10
CLIP = 1.0 - 1e-7
NEG_BIG = -9000000000000000.0
GB = 4
SLOTS = 16
BPW = 3
TILES = 5


def gnn_program(nc, x, adj, weight, bias, node_w, edge_w, W1, out):
    N, D = x.shape
    NB = N // P
    NG = NB // GB
    KD = D // P
    DY = D + 1
    DYP = DY + 3
    CH = 512
    NCH = N // CH
    WORK = 29800
    KEY = 256
    BITS = N // KEY
    UNITS = 2
    UW = N // UNITS
    GT = GB * TILES
    EW = TILES * P
    MASK = -(1 << 23)
    TPC = CH // P

    table_h = nc.dram_tensor("table_h", [N, D], F32, kind="Internal").ap()
    table_y = nc.dram_tensor("table_y", [N, DYP], F32, kind="Internal").ap()

    rows = lambda t: t.rearrange("(b p) d -> p b d", p=P)
    x_r, out_r, th_r, ty_r = rows(x), rows(out), rows(table_h), rows(table_y)

    with ExitStack() as ctx:
        def sb(name, shape, dt=F32):
            return ctx.enter_context(nc.sbuf_tensor(name, shape, dt))

        def sem(name):
            return ctx.enter_context(nc.semaphore(name))

        bank = [ctx.enter_context(nc.psum_tensor(f"bank{i}", [P, CH], F32)) for i in range(8)]

        ident = sb("ident", [P, P])
        rhs_g = sb("rhs_g", [P, KD, DY])
        w0 = sb("w0", [P, KD, D])
        w1 = sb("w1", [P, KD, D])
        bias_bc = sb("bias_bc", [P, D])
        eps_t = sb("eps_t", [P, 1])
        GXW = 3 * D // 2
        gx = sb("gx", [P, NB, GXW])
        gx_b = gx[:, :, :].rearrange("p b c -> p (b c)").bitcast(BF16).rearrange("p (b c) -> p b c", b=NB)
        x1 = gx[:, :, 0:D]
        logit = sb("logit", [P, NB])
        natt = sb("natt", [P, NB])
        alpha = sb("alpha", [P, NB])
        col = sb("col", [P, 24, NB])
        cs = lambda k: col[:, k, :]
        front = sb("front", [P, 3, 2 * GB * D])
        xs = front[:, 0, :].rearrange("p (k b d) -> p k b d", k=2, b=GB)
        hs = front[:, 1, :].rearrange("p (k b d) -> p k b d", k=2, b=GB)
        hT = front[:, 2, :].rearrange("p (k b c n) -> p k b c n", k=2, b=GB, c=KD)
        stats = sb("stats", [P, GB, 6])
        mv = sb("mv", [P, GB, 2])
        std = sb("std", [P, GB])
        rstd = sb("rstd", [P, GB])
        nmr = sb("nmr", [P, GB])
        fs = sb("fs", [P, 2, D])
        work = sb("work", [P, WORK])

        def arena(off, *shape, dt=F32):
            n = 1
            for s in shape:
                n *= s
            words = n if dt == F32 else (n + 1) // 2
            v = work[:, off:off + words]
            if dt != F32:
                v = v.bitcast(dt)
            if len(shape) == 2:
                v = v.rearrange("p (a b) -> p a b", a=shape[0])
            if len(shape) == 3:
                v = v.rearrange("p (a b c) -> p a b c", a=shape[0], b=shape[1])
            return v, off + words

        bar = sem("bar")
        bars = {}

        def barrier(eng):
            n = bars.get(eng, 0) + 1
            bars[eng] = n
            eng.drain().then_inc(bar, 1)
            eng.wait_ge(bar, 5 * n)

        def skewed(eng, a, b, b_first=False):
            a(0, 0)
            with eng.Fori(0, NG // 2 - 1) as j:
                for k in (0, 1):
                    g = 2 * j + k
                    if b_first:
                        b(g, k)
                        a(g + 1, 1 - k)
                    else:
                        a(g + 1, 1 - k)
                        b(g, k)
            if b_first:
                b(NG - 2, 0)
                a(NG - 1, 1)
            else:
                a(NG - 1, 1)
                b(NG - 2, 0)
            b(NG - 1, 1)

        grp = lambda g: bass.ds(g * GB, GB) if not isinstance(g, int) else slice(g * GB, g * GB + GB)
        at = lambda b, n=1: bass.ds(b, n) if not isinstance(b, int) else slice(b, b + n)

        class Front:
            def __init__(self, t):
                self.x_in = [sem(f"{t}_x_in0"), sem(f"{t}_x_in1")]
                self.x_used = sem(f"{t}_x_used")
                self.var = sem(f"{t}_var")
                self.sqrt = sem(f"{t}_sqrt")
                self.rstd = sem(f"{t}_rstd")
                self.h = sem(f"{t}_h")
                self.t = sem(f"{t}_t")
                self.hT = sem(f"{t}_hT")
                self.prod = sem(f"{t}_prod")
                self.prod_used = sem(f"{t}_prod_used")

        f0 = Front("f0")
        f1 = Front("f1")

        def front_stats(d, f, src, g):
            for b in range(GB):
                d.bn_stats(stats[:, b, :], src[:, b, :])
            d.drain()
            for b in range(GB):
                d.bn_aggr(mv[:, b, :], stats[:, b, :])
            d.drain().then_inc(f.var, 1)
            d.wait_ge(f.sqrt, g + 1)
            d.reciprocal(rstd[:, :], std[:, :])
            d.drain()
            d.scalar_tensor_tensor(nmr[:, :], mv[:, :, 0], -1.0, rstd[:, :], ALU.mult, ALU.mult)
            d.drain().then_inc(f.rstd, 1)

        def front_norm(a, f, src, g, k):
            a.wait_ge(f.var, g + 1)
            a.activation(std[:, :], mv[:, :, 1], ACT.Sqrt, bias=eps_t[:, 0:1])
            a.drain().then_inc(f.sqrt, 1)
            a.wait_ge(f.rstd, g + 1)
            a.wait_ge(f.t, GB * (g + 1))
            for b in range(GB):
                a.activation(hs[:, k, b, :], src[:, b, :], ACT.Relu, bias=nmr[:, b:b + 1],
                             scale=rstd[:, b:b + 1]).then_inc(f.h, 1)

        def front_transpose(t, f, g, k):
            t.wait_ge(f.hT, g + 1)
            for b in range(GB):
                t.wait_ge(f.h, GB * g + b + 1)
                for c in range(KD):
                    last = t.transpose(bank[b // 2][:, ((b % 2) * KD + c) * P:((b % 2) * KD + c + 1) * P],
                                       hs[:, k, b, c * P:(c + 1) * P], ident[:, :])
                last.then_inc(f.t, 1)

        def front_hT(d, f, g, k):
            d.wait_ge(f.prod, GB * (g + 1))
            for j in range(GB // 2):
                d.wait_ge(f.t, GB * (g + 2) + 2 * j + 2)
                d.tensor_copy(hT[:, k, 2 * j:2 * j + 2, :, :].rearrange("p b c n -> p (b c n)"), bank[j][:, :])
            d.drain().then_inc(f.hT, 1)

        def front_product(t, f, rhs, n, g, k):
            t.wait_ge(f.hT, g + 2)
            t.wait_ge(f.prod_used, g + 1)
            for b in range(GB):
                for c in range(KD):
                    last = t.matmul(bank[2 + b][:, 0:n], hT[:, k, b, c, :], rhs[:, c, 0:n],
                                    start=(c == 0), stop=(c == KD - 1))
                last.then_inc(f.prod, 1)

        ew, o = arena(2 * N, KD, D)
        ewT, o = arena(o, KD, D)
        res, o = arena(o, 2, GB, D)
        nw, o = arena(o, KD)

        s_w = sem("s_w")
        s_ident = sem("s_ident")
        s_ewT = sem("s_ewT")
        s_ewTc = sem("s_ewTc")
        s_eet = sem("s_eet")
        s_hi = sem("s_hi")
        s_rest = sem("s_rest")
        s_restfree = sem("s_restfree")
        s_th = sem("s_th")
        s_red = sem("s_red")
        s_all = sem("s_all")
        s_stored = sem("s_stored")
        s_exp = sem("s_exp")
        s_negmax = sem("s_negmax")

        hn, o = arena(0, NB, D)
        hnT, o = arena(o, KD, N)
        em, o = arena(o, N)
        ad, o = arena(o, N)
        pt, o = arena(o, 2, CH)
        stg, o = arena(o, D)
        gT, o = arena(o, KD, P)
        xr, o = arena(o, D)
        ag, o = arena(o, D)
        agT, o = arena(o, KD, P)
        sc, o = arena(o, 8)
        assert o <= WORK, o
        A = {n: sem("ga_" + n) for n in (
            "hn", "staged", "stage_free", "setT", "setTc", "adj", "x", "done", "gT", "gTc", "scores",
            "masked", "max", "exp", "weights", "pt", "ptc", "agg", "aggc", "aggT", "aggTc", "proj")}

        def ga_sp(e):
            e.dma_start(hn, th_r).then_inc(A["hn"], 16)
            with e.Fori(0, NB) as i:
                e.wait_ge(A["done"], i + 1)
                e.dma_start(ad, adj[bass.ds(i * P, P), :]).then_inc(A["adj"], 16)
                e.dma_start(xr, x[bass.ds(i * P, P), :]).then_inc(A["x"], 16)
            e.wait_ge(A["done"], NB + 1)

        def ga_dve(d):
            d.sem_inc(A["done"], 1)
            d.sem_inc(A["masked"], 2)
            d.wait_ge(A["hn"], 16)
            with d.Fori(0, NB) as t:
                d.wait_ge(A["stage_free"], t + 1)
                d.tensor_copy(stg, hn[:, bass.ds(t, 1), :])
                d.drain().then_inc(A["staged"], 1)
            with d.Fori(0, NB) as i:
                d.wait_ge(A["adj"], 16 * (i + 1))
                d.tensor_scalar(em, ad, 0.0, NEG_BIG, ALU.is_le, ALU.mult)
                d.drain()
                for c in range(NCH):
                    d.wait_ge(A["scores"], NCH * i + c + 1)
                    d.tensor_tensor(em[:, c * CH:(c + 1) * CH], em[:, c * CH:(c + 1) * CH],
                                    bank[c % 2][:, :], ALU.add).then_inc(A["masked"], 1)
                d.drain()
                d.tensor_reduce(sc[:, 0:1], em, AX, ALU.max)
                d.drain()
                d.tensor_scalar(sc[:, 1:2], sc[:, 0:1], -1.0, None, ALU.mult)
                d.drain().then_inc(A["max"], 1)
                d.wait_ge(A["exp"], i + 1)
                d.tensor_tensor(em, em, ad, ALU.mult)
                d.drain().then_inc(A["weights"], 1)
                d.reciprocal(sc[:, 3:4], sc[:, 2:3])
                d.wait_ge(A["x"], 16 * (i + 1))
                d.tensor_tensor(xr, xr, bias_bc[:, :], ALU.add)
                d.drain()
                d.tensor_tensor(sc[:, 4:5], sc[:, 3:4], natt[:, bass.ds(i, 1)], ALU.mult)
                d.drain()
                d.wait_ge(A["proj"], i + 1)
                d.scalar_tensor_tensor(x1[:, bass.ds(i, 1), :], bank[7][:, 0:D], sc[:, 4:5], xr, ALU.mult, ALU.add)
                d.drain().then_inc(A["done"], 1)

        def ga_pe(t):
            t.sem_inc(A["stage_free"], 1)
            with t.Fori(0, NB) as i:
                t.wait_ge(A["staged"], i + 1)
                t.wait_ge(A["setTc"], i + 1)
                for c in range(KD):
                    last = t.transpose(bank[2][:, c * P:(c + 1) * P], stg[:, c * P:(c + 1) * P], ident[:, :])
                t.drain().then_inc(A["stage_free"], 1)
                t.sem_inc(A["setT"], 1)
            t.wait_ge(A["setTc"], NB + 1)
            with t.Fori(0, NB) as i:
                for r in range(KD):
                    for c in range(KD):
                        last = t.matmul(bank[2][:, r * P:(r + 1) * P], rhs_g[:, c, r * P:(r + 1) * P],
                                        hnT[:, c, bass.ds(i * P, P)], start=(c == 0), stop=(c == KD - 1))
                last.then_inc(A["gT"], 1)
                t.wait_ge(A["gTc"], i + 1)
                for c in range(NCH):
                    t.wait_ge(A["masked"], NCH * i + c + 1)
                    for k in range(KD):
                        last = t.matmul(bank[c % 2][:, :], gT[:, k, :], hnT[:, k, c * CH:(c + 1) * CH],
                                        start=(k == 0), stop=(k == KD - 1))
                    last.then_inc(A["scores"], 1)
                t.wait_ge(A["weights"], i + 1)

                def add_chunk(c):
                    t.wait_ge(A["ptc"], NCH * i + c + 1)
                    for q in range(TPC):
                        n = c * TPC + q
                        last = t.matmul(bank[5][:, 0:D], pt[:, c % 2, q * P:(q + 1) * P], hn[:, n, :],
                                        start=(n == 0), stop=(n == NB - 1))
                    return last

                for c in range(NCH):
                    for q in range(TPC):
                        n = c * TPC + q
                        last = t.transpose(bank[3 + c % 2][:, q * P:(q + 1) * P], em[:, n * P:(n + 1) * P],
                                           ident[:, :])
                    last.then_inc(A["pt"], 1)
                    if c:
                        add_chunk(c - 1)
                add_chunk(NCH - 1).then_inc(A["agg"], 1)
                t.wait_ge(A["aggc"], i + 1)
                for k in range(KD):
                    last = t.transpose(bank[6][:, k * P:(k + 1) * P], ag[:, k * P:(k + 1) * P], ident[:, :])
                last.then_inc(A["aggT"], 1)
                t.wait_ge(A["aggTc"], i + 1)
                for k in range(KD):
                    last = t.matmul(bank[7][:, 0:D], agT[:, k, :], w0[:, k, :], start=(k == 0), stop=(k == KD - 1))
                last.then_inc(A["proj"], 1)

        def ga_act(a):
            a.sem_inc(A["setTc"], 1)
            with a.Fori(0, NB) as t:
                a.wait_ge(A["setT"], t + 1)
                for c in range(KD):
                    a.activation(hnT[:, c, bass.ds(t * P, P)], bank[2][:, c * P:(c + 1) * P], ACT.Copy)
                a.drain().then_inc(A["setTc"], 1)
            with a.Fori(0, NB) as i:
                a.wait_ge(A["gT"], i + 1)
                a.activation(gT.rearrange("p a b -> p (a b)"), bank[2][:, 0:D], ACT.Copy).then_inc(A["gTc"], 1)
                a.wait_ge(A["max"], i + 1)
                a.activation(em, em, ACT.Exp, bias=sc[:, 1:2], accum_out=sc[:, 2:3]).then_inc(A["exp"], 1)
                for c in range(NCH):
                    a.wait_ge(A["pt"], NCH * i + c + 1)
                    a.activation(pt[:, c % 2, :], bank[3 + c % 2][:, :], ACT.Copy).then_inc(A["ptc"], 1)
                a.wait_ge(A["agg"], i + 1)
                a.activation(ag, bank[5][:, 0:D], ACT.Copy).then_inc(A["aggc"], 1)
                a.wait_ge(A["aggT"], i + 1)
                a.activation(agT.rearrange("p a b -> p (a b)"), bank[6][:, 0:D], ACT.Copy).then_inc(A["aggTc"], 1)

        adu, o = arena(0, 2, UNITS, UW)
        abf, o = arena(o, UNITS, UW, dt=BF16)
        gat, o = arena(o, 2 * GT, D)
        gat = gat.rearrange("p (k n) d -> p k n d", k=2)
        key, o = arena(o, 2, KEY)
        wid, o = arena(o, BITS, P, dt=BF16)
        idb = wid[:, 0, :]
        upper, o = arena(o, P, dt=BF16)
        iow, o = arena(o, EW, dt=F16)
        iok, o = arena(o, KEY)
        posc, o = arena(o, TILES)
        t16, o = arena(o, 2, GB, SLOTS)
        ia, o = arena(o, GB, SLOTS)
        ib, o = arena(o, GB, SLOTS)
        wf, o = arena(o, GB, SLOTS)
        cf, o = arena(o, GB, SLOTS)
        tp, o = arena(o, GB, SLOTS)
        r1, o = arena(o, GB, SLOTS)
        e48, o = arena(o, GB, BPW * SLOTS)
        s16, o = arena(o, GB, SLOTS)
        nv, o = arena(o, 2, GB)
        nvb, o = arena(o, GB, dt=BF16)
        cnt, o = arena(o, 2, GB, UNITS)
        ends, o = arena(o, 2, GB)
        vt, o = arena(o, GB, 2 * SLOTS + 2, dt=F16)
        oh, o = arena(o, 2 * GT, SLOTS)
        oh = oh.rearrange("p (k n) s -> p k n s", k=2)
        rr, o = arena(o, GT)
        jt, o = arena(o, GT, SLOTS)
        jj, o = arena(o, GT)
        ixf, o = arena(o, 2, GT)
        ee, o = arena(o, 2, GT)
        e3, o = arena(o, GT, 4, dt=BF16)
        ohe, o = arena(o, GT * 3, SLOTS, dt=BF16)
        ohe = ohe.rearrange("p (n q) s -> p n q s", q=3)
        es, o = arena(o, GB, SLOTS)
        sm, o = arena(o, 6, GB)
        pr, o = arena(o, 2, GB, SLOTS)
        p3, o = arena(o, GB * 3, SLOTS, dt=BF16)
        p3 = p3.rearrange("p (b q) s -> p b q s", q=3)
        pe_, o = arena(o, GT)
        aT, o = arena(o, 2, KD, P)
        ot, o = arena(o, GT, P, dt=BF16)
        am1, o = arena(o, EW, dt=BF16)
        assert o <= WORK, o
        xr2 = xs
        flat = front[:, :, :].rearrange("p a n -> p (a n)")
        am = flat[:, 2 * GB * D:2 * GB * D + GB * EW].bitcast(BF16).rearrange("p (k b e) -> p k b e", k=2, b=GB)
        otp = flat[:, 2 * GB * D + GB * EW:2 * GB * D + GB * EW + 2 * EW].rearrange("p (k q n) -> p k q n", k=2, q=TILES)
        junk = fs[:, :, :]
        idx = sb("idx", [P, NB * TILES], I32)
        first_e = sb("first_e", [P, NB])
        last_e = sb("last_e", [P, NB])
        bad = sb("bad", [P, NB])
        badc = sb("badc", [P, 2])
        pdum = sb("pdum", [P, 1])
        flag = sb("flag", [P, 1], I32)
        t6b = bank[6][:, :].bitcast(BF16)

        L = {n: sem("fa_" + n) for n in (
            "conv",
            "pack",
            "key",
            "nv",
            "start",
            "m",
            "v",
            "idx",
            "x",
            "xb",
            "ott",
            "otc",
            "exp_g",
            "dot",
            "ohe",
            "es",
            "smax",
            "pexp",
            "p3",
            "pb",
            "otp",
            "agg",
            "aggc",
            "proj",
            "x1",
            "flag1")}
        L["adj"] = [[sem(f"fa_adj{n}{h}") for h in range(UNITS)] for n in range(2)]
        L["gat"] = [[sem(f"fa_gat{k}{b}") for b in range(GB)] for k in range(2)]

        def fast_constants(p):
            p.iota(iow, pattern=[[1, EW]], base=0, channel_multiplier=0, allow_small_or_imprecise_dtypes=True)
            p.iota(iok, pattern=[[1, KEY]], base=0, channel_multiplier=0, allow_small_or_imprecise_dtypes=True)
            p.iota(posc, pattern=[[P, TILES]], base=0, channel_multiplier=1, allow_small_or_imprecise_dtypes=True)
            p.memset(wid, 0.0)
            p.memset(upper, 1.0)
            p.memset(bad[:, :], 0.0)
            p.drain()
            for m in range(BITS):
                p.affine_select(out=wid[:, m, :], in_=wid[:, m, :], compare_op=ALU.not_equal, fill=float(1 << m),
                                base=0, pattern=[[-1, P]], channel_multiplier=1)
            p.affine_select(out=upper, in_=upper, compare_op=ALU.is_gt, fill=0.0, base=0, pattern=[[1, P]],
                            channel_multiplier=-1)
            p.drain()

        def staged(eng, body):
            body((0, 0), None, None)
            body((1, 1), (0, 0), None)
            with eng.Fori(0, (NG - 2) // 2) as j:
                for k in (0, 1):
                    g = 2 * j + k
                    body((g + 2, k), (g + 1, 1 - k), (g, k))
            body(None, (NG - 1, 1), (NG - 2, 0))
            body(None, None, (NG - 1, 1))

        def fast_load(e):
            with e.Fori(0, (NB - 2) // 2) as j:
                for n in range(2):
                    for h in range(UNITS):
                        e.wait_ge(L["conv"], 2 * UNITS * j + UNITS * n + h + 1)
                        e.dma_start(adu[:, n, h, :], adj[bass.ds((2 * j + 2 + n) * P, P), h * UW:(h + 1) * UW]) \
                            .then_inc(L["adj"][n][h], 16)

        def fast_act(a):
            a.sem_inc(L["otc"], 1)
            a.sem_inc(L["aggc"], GB)

            def body(wd, ls, at_):
                for b in range(GB):
                    if wd:
                        g, k = wd
                        if b == 0 and not isinstance(g, int):
                            a.wait_ge(L["nv"], g - 1)
                        for h in range(UNITS):
                            a.wait_ge(L["adj"][b % 2][h], 16 * (2 * g + b // 2 + 1))
                            a.wait_ge(L["pack"], UNITS * GB * g + UNITS * b + h + 1)
                            a.activation(abf[:, h, :], adu[:, b % 2, h, :], ACT.Copy,
                                         accum_out=cnt[:, k, b, h:h + 1]).then_inc(L["conv"], 1)
                    if at_:
                        g, k = at_
                        if b == 0:
                            a.wait_ge(L["otp"], GB * g + GB)
                        a.wait_ge(L["ott"], GB * g + b + 1)
                        a.activation(ot[:, b * TILES:(b + 1) * TILES, :],
                                     t6b[:, 0:EW].rearrange("p (q n) -> p q n", q=TILES),
                                     ACT.Copy).then_inc(L["otc"], 1)
                if at_:
                    g, k = at_
                    a.wait_ge(L["smax"], g + 1)
                    a.activation(pr[:, 0, :, :], es, ACT.Exp).then_inc(L["pexp"], 1)
                    for b in range(GB):
                        a.wait_ge(L["agg"], GB * g + b + 9)
                        a.wait_ge(L["proj"], GB * g + b + 1)
                        a.activation(aT[:, b % 2, :, :].rearrange("p c n -> p (c n)"), bank[4 + b % 2][:, 0:D],
                                     ACT.Copy).then_inc(L["aggc"], 1)
            staged(a, body)

        def fast_pool(p):
            def body(wd, ls, at_):
                if ls:
                    g, k = ls
                    p.wait_ge(L["x1"], GB * g + GB)
                    p.dma_start(xr2[:, k, :, :], x_r[:, grp(g), :]).then_inc(L["x"], 16)
                    p.wait_ge(L["agg"], GB * g + GB)
                    p.wait_ge(L["idx"], g + 1)
                    p.tensor_tensor(pdum[:, :], eps_t[:, :], eps_t[:, :], ALU.add)
                    p.drain()
                    for n in range(GT):
                        p.indirect_dma_start(gat[:, k, n, :], None, table_h,
                                             bass.IndirectOffsetOnAxis(ix[:, k, n:n + 1], 0)) \
                            .then_inc(L["gat"][k][n // TILES], 16)
                    p.wait_ge(L["x"], 16 * (g + 1))
                    for b in range(GB):
                        p.tensor_tensor(xr2[:, k, b, :], xr2[:, k, b, :], bias_bc[:, :], ALU.add)
                    p.drain().then_inc(L["xb"], 1)
            staged(p, body)

        ix = ixf.bitcast(I32)

        def fast_flag(p):
            p.wait_ge(L["flag1"], 1)
            p.partition_all_reduce(badc[:, 1:2], badc[:, 0:1], P, RMAX)
            p.drain()
            p.tensor_copy(flag[:, :], badc[:, 1:2])
            p.drain()

        def general_if(eng, general=None, fast=None):
            f = eng.value_load(flag[0:1, 0:1], min_val=0, max_val=1)
            with eng.If(f > 0):
                if general:
                    general(eng)
                eng.nop()
            with eng.Else():
                if fast:
                    fast(eng)
                eng.nop()

        def fast_pe(t):
            t.sem_inc(L["pack"], UNITS)
            t.sem_inc(L["agg"], 2 * GB)
            t.sem_inc(L["proj"], 2)

            def body(wd, ls, at_):
                for b in range(GB):
                    if at_:
                        g, k = at_
                        t.wait_ge(L["otc"], GB * g + b + 1)
                        for q in range(TILES):
                            last = t.transpose(t6b[:, q * P:(q + 1) * P], am[:, k, b, q * P:(q + 1) * P], idb)
                        last.then_inc(L["ott"], 1)
                        if b == 0:
                            t.wait_ge(L["aggc"], GB * g + GB)
                        for q in range(TILES):
                            n = b * TILES + q
                            t.wait_ge(L["dot"], GT * g + n + 1)
                            for c in range(3):
                                last = t.matmul(bank[4 + n % 2][:, 0:D], am[:, k, b, q * P:(q + 1) * P],
                                                gx_b[:, at(g * GB + b), c * D:(c + 1) * D],
                                                start=(c == 0), stop=(c == 2))
                            last.then_inc(L["exp_g"], 1)
                    if wd:
                        g, k = wd
                        t.wait_ge(L["key"], GB * g + b + 1)
                        for h in range(UNITS):
                            t.wait_ge(L["conv"], UNITS * GB * g + UNITS * b + h + 1)
                            for m in range(BITS // UNITS):
                                mm = h * BITS // UNITS + m
                                last = t.matmul(bank[b % 2][:, 0:KEY], wid[:, mm, :],
                                                abf[:, h, m * KEY:(m + 1) * KEY],
                                                start=(mm == 0), stop=(mm == BITS - 1))
                            last.then_inc(L["pack"], 1)
                if ls:
                    g, k = ls
                    t.wait_ge(L["nv"], g + 1)
                    t.wait_ge(L["x1"], GB * g + GB)
                    t.matmul(bank[7][:, 0:GB], upper, nvb, start=True, stop=True).then_inc(L["start"], 1)
                    for b in range(GB):
                        t.wait_ge(L["m"], GB * g + b + 1)
                        for q in range(TILES):
                            last = t.matmul(bank[2 + b // 2][:, ((b % 2) * TILES + q) * 33:
                                                             ((b % 2) * TILES + q) * 33 + 33],
                                            am[:, k, b, q * P:(q + 1) * P], vt[:, b, 0:33], start=True, stop=True)
                        if b % 2:
                            last.then_inc(L["v"], 1)
                if at_:
                    g, k = at_
                    t.wait_ge(L["ohe"], g + 1)
                    t.wait_ge(L["otc"], GB * g + GB + 1)
                    t.wait_ge(L["x1"], GB * g + 2 * GB)
                    for b in range(GB):
                        for q in range(TILES):
                            n = b * TILES + q
                            last = t.matmul(bank[7][:, b * 48:b * 48 + 48], ot[:, n, :],
                                            ohe[:, n, :, :].rearrange("p q s -> p (q s)"),
                                            start=(q == 0), stop=(q == TILES - 1))
                    last.then_inc(L["es"], 1)
                    t.wait_ge(L["p3"], g + 1)
                    if ls:
                        t.wait_ge(L["idx"], g + 2)
                    for b in range(GB):
                        for q in range(TILES):
                            n = (b % 2) * TILES + q
                            last = t.matmul(bank[2 + b // 2][:, n * 48:n * 48 + 48], am[:, k, b, q * P:(q + 1) * P],
                                            p3[:, b, :, :].rearrange("p q s -> p (q s)"), start=True, stop=True)
                        if b % 2:
                            last.then_inc(L["pb"], 1)

                    def proj(b):
                        t.wait_ge(L["aggc"], GB * g + GB + b + 1)
                        t.wait_ge(L["x1"], GB * g + 2 * GB + b)
                        for c in range(KD):
                            last = t.matmul(bank[7][:, 0:D], aT[:, b % 2, c, :], w0[:, c, :],
                                            start=(c == 0), stop=(c == KD - 1))
                        last.then_inc(L["proj"], 1)

                    for b in range(GB):
                        t.wait_ge(L["gat"][k][b], 8 * TILES * (g - k) + 16 * TILES)
                        t.wait_ge(L["otp"], GB * g + GB + b + 1)
                        if b >= 2:
                            t.wait_ge(L["aggc"], GB * g + b + 3)
                        for c in range(KD):
                            for q in range(TILES):
                                last = t.matmul(bank[4 + b % 2][:, c * P:(c + 1) * P],
                                                gat[:, k, b * TILES + q, c * P:(c + 1) * P], otp[:, b % 2, q, :],
                                                start=(q == 0), stop=(q == TILES - 1))
                        last.then_inc(L["agg"], 1)
                        if b:
                            proj(b - 1)
                    proj(GB - 1)
            staged(t, body)

        def fast_dve(d):
            d.sem_inc(L["key"], 2)
            d.sem_inc(L["dot"], 2)
            d.sem_inc(L["otp"], GB)
            d.sem_inc(L["x1"], 2 * GB)
            bc = lambda v, shape, axis: v.unsqueeze(axis).broadcast_to(shape)

            def keys(g, k, pair):
                bs = (2 * pair, 2 * pair + 1)
                for b in bs:
                    d.wait_ge(L["pack"], UNITS * GB * g + UNITS * (b + 1) + UNITS)
                    d.scalar_tensor_tensor(key[:, b % 2, :], bank[b % 2][:, 0:KEY], float(KEY), iok, ALU.mult,
                                           ALU.add).then_inc(L["key"], 1)
                d.drain()
                for b in bs:
                    d.max(t16[:, k, b, 0:8], key[:, b % 2, :])
                d.drain()
                for b in bs:
                    d.match_replace(key[:, b % 2, :], t16[:, k, b, 0:8], key[:, b % 2, :], -1.0)
                d.drain()
                for b in bs:
                    d.max(t16[:, k, b, 8:16], key[:, b % 2, :])
                d.drain()

            def edge_list(g, k):
                ti, tw = ia.bitcast(I32), ib.bitcast(I32)
                then(d, d.tensor_copy(ti, t16[:, k, :, :]))
                then(d, d.tensor_scalar(tw, ti, 8, None, ALU.logical_shift_right))
                then(d, d.tensor_scalar(ti, ti, KEY - 1, None, ALU.bitwise_and))
                d.tensor_copy(wf, tw)
                then(d, d.tensor_copy(cf, ti))
                then(d, d.tensor_scalar(tp.bitcast(I32), wf.bitcast(I32), MASK, None, ALU.bitwise_and))
                for v in range(BPW):
                    if v + 1 < BPW:
                        d.tensor_tensor(r1, (wf, r1)[v > 0], tp, ALU.subtract)
                    then(d, d.scalar_tensor_tensor(e48[:, :, v * SLOTS:(v + 1) * SLOTS], tp, float(KEY), cf,
                                                   ALU.mult, ALU.add))
                    if v + 1 < BPW:
                        then(d, d.tensor_scalar(tp.bitcast(I32), r1.bitcast(I32), MASK, None, ALU.bitwise_and))
                for b in range(GB):
                    d.max(s16[:, b, 0:8], e48[:, b, :])
                d.drain()
                for b in range(GB):
                    d.match_replace(e48[:, b, :], s16[:, b, 0:8], e48[:, b, :], -1.0)
                d.drain()
                for b in range(GB):
                    d.max(s16[:, b, 8:16], e48[:, b, :])
                d.drain()
                d.tensor_scalar(wf, s16, float(KEY), None, ALU.is_ge)
                then(d, d.tensor_copy(ti, s16))
                d.tensor_reduce(nv[:, k, :], wf, AX, ALU.add)
                then(d, d.tensor_scalar(tw, ti, 8, None, ALU.logical_shift_right))
                d.tensor_copy(nvb, nv[:, k, :])
                d.tensor_reduce(alpha[:, grp(g)], cnt[:, k, :, :], AX, ALU.add)
                d.drain().then_inc(L["nv"], 1)
                then(d, d.tensor_scalar(ti, ti, KEY - 1, None, ALU.bitwise_and))
                then(d, d.tensor_copy(tp, tw))
                d.tensor_copy(vt[:, :, SLOTS:2 * SLOTS], ti)
                then(d, d.tensor_scalar(tw, tp.bitcast(I32), 23, None, ALU.logical_shift_right))
                d.tensor_copy(vt[:, :, 0:SLOTS], tw)
                d.tensor_tensor(sm[:, 5, :], alpha[:, grp(g)], nv[:, k, :], ALU.not_equal)
                d.wait_ge(L["start"], g + 1)
                then(d, d.tensor_copy(ends[:, 0, :], bank[7][:, 0:GB]))
                d.tensor_copy(vt[:, :, 2 * SLOTS:2 * SLOTS + 1].rearrange("p b o -> p (b o)"), ends[:, 0, :])
                then(d, d.tensor_tensor(ends[:, 1, :], ends[:, 0, :], nv[:, k, :], ALU.add))
                d.tensor_copy(first_e[:, grp(g)], ends[:, 0, :])
                d.tensor_copy(last_e[:, grp(g)], ends[:, 1, :])
                d.scalar_tensor_tensor(bad[:, grp(g)], ends[:, 1, :], float(EW), sm[:, 5, :], ALU.is_gt, ALU.max)
                for b in range(GB):
                    then(d, d.tensor_scalar(am1, iow, ends[:, 1, b:b + 1], None, ALU.is_lt))
                    d.scalar_tensor_tensor(am[:, k, b, :], iow, ends[:, 0, b:b + 1], am1, ALU.is_ge, ALU.mult)
                    d.drain().then_inc(L["m"], 1)
                for v in range(2):
                    half = slice(v * GT // 2, (v + 1) * GT // 2)
                    sel = bank[2 + v][:, 0:33 * GT // 2].rearrange("p (n s) -> p n s", s=33)
                    d.wait_ge(L["v"], 2 * g + v + 1)
                    d.tensor_tensor(rr[:, half].rearrange("p (b q) -> p b q", q=TILES), bc(posc, [P, 2, TILES], 1),
                                    sel[:, :, 32].rearrange("p (b q) -> p b q", q=TILES), ALU.subtract)
                    d.tensor_copy(jt[:, half, :], sel[:, :, SLOTS:2 * SLOTS])
                    d.drain()
                    d.scalar_tensor_tensor(jt[:, half, :], sel[:, :, 0:SLOTS], float(KEY), jt[:, half, :], ALU.mult,
                                           ALU.add)
                then(d, d.tensor_tensor(oh[:, k, :, :], bc(iok[:, 0:SLOTS], [P, GT, SLOTS], 1),
                                        bc(rr, [P, GT, SLOTS], 2), ALU.is_equal))
                then(d, d.tensor_tensor(jt, jt, oh[:, k, :, :], ALU.mult))
                then(d, d.tensor_reduce(jj, jt, AX, ALU.add))
                then(d, d.tensor_scalar(jj, jj, float(127 * KEY + N - 1), float(127 * KEY), ALU.min, ALU.subtract))
                then(d, d.tensor_scalar(ix[:, k, :], jj, 0.0, None, ALU.max))
                d.tensor_copy(idx[:, bass.ds(g * GT, GT) if not isinstance(g, int) else slice(g * GT, g * GT + GT)],
                              ix[:, k, :])
                d.drain().then_inc(L["idx"], 1)

            def dots(g, k, b):
                d.wait_ge(L["gat"][k][b], 8 * TILES * (g - k) + 16 * TILES)
                for q in range(TILES):
                    n = b * TILES + q
                    d.wait_ge(L["exp_g"], GT * g + n + 1)
                    d.tensor_tensor_reduce(out=junk[:, n % 2, :], in0=gat[:, k, n, :], in1=bank[4 + n % 2][:, 0:D],
                                           scale=1.0, scalar=0.0, op0=ALU.mult, op1=ALU.add,
                                           accum_out=ee[:, 0, n:n + 1]).then_inc(L["dot"], 1)

            def scores(g, k):
                d.drain()
                e = ee[:, 0, :]
                r = ee[:, 1, :]
                then(d, d.tensor_copy(e3[:, :, 0], e))
                then(d, d.tensor_tensor(r, e, e3[:, :, 0], ALU.subtract))
                then(d, d.tensor_copy(e3[:, :, 1], r))
                then(d, d.tensor_tensor(e3[:, :, 2], r, e3[:, :, 1], ALU.subtract))
                d.tensor_tensor(ohe, bc(oh[:, k, :, :], [P, GT, 3, SLOTS], 2),
                                bc(e3[:, :, 0:3], [P, GT, 3, SLOTS], 3), ALU.mult)
                d.drain().then_inc(L["ohe"], 1)
                sp = bank[7][:, 0:GB * 48].rearrange("p (b q s) -> p b q s", b=GB, q=3)
                then(d, d.tensor_tensor(pr[:, 1, :, :], bc(iok[:, 0:SLOTS], [P, GB, SLOTS], 1),
                                        bc(nv[:, k, :], [P, GB, SLOTS], 2), ALU.is_ge))
                d.wait_ge(L["es"], g + 1)
                then(d, d.scalar_tensor_tensor(es, pr[:, 1, :, :], -1e30, sp[:, :, 2, :], ALU.mult, ALU.add))
                then(d, d.tensor_tensor(es, es, sp[:, :, 1, :], ALU.add))
                then(d, d.tensor_tensor(es, es, sp[:, :, 0, :], ALU.add))
                then(d, d.tensor_reduce(sm[:, 0, :], es, AX, ALU.max))
                d.tensor_tensor(es, es, bc(sm[:, 0, :], [P, GB, SLOTS], 2), ALU.subtract)
                d.drain().then_inc(L["smax"], 1)
                d.wait_ge(L["pexp"], g + 1)
                pf, pq = pr[:, 0, :, :], pr[:, 1, :, :]
                d.tensor_reduce(sm[:, 1, :], pf, AX, ALU.add)
                then(d, d.tensor_copy(p3[:, :, 0, :], pf))
                then(d, d.tensor_tensor(pq, pf, p3[:, :, 0, :], ALU.subtract))
                then(d, d.tensor_copy(p3[:, :, 1, :], pq))
                d.tensor_tensor(p3[:, :, 2, :], pq, p3[:, :, 1, :], ALU.subtract)
                d.drain().then_inc(L["p3"], 1)
                then(d, d.reciprocal(sm[:, 2, :], sm[:, 1, :]))
                d.tensor_tensor(sm[:, 3, :], sm[:, 2, :], natt[:, grp(g)], ALU.mult)
                for v in range(2):
                    half = slice(v * GT // 2, (v + 1) * GT // 2)
                    sel = bank[2 + v][:, 0:48 * GT // 2].rearrange("p (n q s) -> p n q s", q=3, s=SLOTS)
                    d.wait_ge(L["pb"], 2 * g + v + 1)
                    then(d, d.tensor_tensor(jt[:, half, :], sel[:, :, 2, :], oh[:, k, half, :], ALU.mult))
                    for q in (1, 0):
                        then(d, d.tensor_tensor(pbt, sel[:, :, q, :], oh[:, k, half, :], ALU.mult))
                        then(d, d.tensor_tensor(jt[:, half, :], jt[:, half, :], pbt, ALU.add))
                then(d, d.tensor_reduce(pe_, jt, AX, ALU.add))
                for b in range(GB):
                    d.wait_ge(L["agg"], GB * g + b + 7)
                    for q in range(TILES):
                        n = b * TILES + q
                        d.tensor_scalar(otp[:, b % 2, q, :], ot[:, n, :], pe_[:, n:n + 1], None, ALU.mult)
                    d.drain().then_inc(L["otp"], 1)
                    if b:
                        new_x(g, k, b - 1)
                new_x(g, k, GB - 1)

            def new_x(g, k, b):
                d.wait_ge(L["xb"], g + 1)
                d.wait_ge(L["proj"], GB * g + b + 3)
                d.scalar_tensor_tensor(x1[:, at(g * GB + b), :], bank[7][:, 0:D], sm[:, 3, b:b + 1],
                                       xr2[:, k, b, :], ALU.mult, ALU.add).then_inc(L["x1"], 1)

            def body(wd, ls, at_):
                for pair in range(2):
                    if at_:
                        dots(*at_, 2 * pair)
                        dots(*at_, 2 * pair + 1)
                    if wd:
                        keys(*wd, pair)
                if ls:
                    edge_list(*ls)
                if at_:
                    scores(*at_)
            staged(d, body)
            d.drain()
            then(d, d.tensor_reduce(badc[:, 0:1], bad[:, :], AX, ALU.max))
            d.drain().then_inc(L["flag1"], 1)

        pbt = junk[:, :, :].rearrange("p a b -> p (a b)")[:, 0:GT // 2 * SLOTS].rearrange("p (n s) -> p n s", s=SLOTS)

        mx, o = arena(0, NB, D)
        ys, o = arena(o, 2, GB, DYP)
        assert o <= WORK, o
        s_mx = sem("s_mx")
        s_sq = sem("s_sq")
        s_ys = sem("s_ys")
        s_gm = sem("s_gm")
        s_ysz = sem("s_ysz")
        s_tyo = [sem("s_tyo0"), sem("s_tyo1")]
        s_cc = sem("s_cc")
        s_cd = sem("s_cd")

        s_asked = sem("s_asked")
        s_answered = sem("s_answered")
        asked, answered = [0], [0]

        def ask(d):
            asked[0] += 1
            d.drain().then_inc(s_asked, 1)
            d.wait_ge(s_answered, asked[0])

        def answer(a, o_, i_, func):
            answered[0] += 1
            a.wait_ge(s_asked, answered[0])
            a.activation(o_, i_, func)
            a.drain().then_inc(s_answered, 1)

        def then(d, ins):
            d.drain()

        def root(d, i_):
            d.tensor_scalar(i_, i_, EPS * EPS, None, ALU.max)
            ask(d)

        def artanh(d, o_, i_, y, u, t):
            then(d, d.tensor_scalar(y, i_, CLIP, None, ALU.min))
            then(d, d.tensor_scalar(u, y, -1.0, 1.0, ALU.mult, ALU.add))
            then(d, d.reciprocal(t, u))
            then(d, d.scalar_tensor_tensor(y, y, 2.0, t, ALU.mult, ALU.mult))
            d.tensor_scalar(u, y, 1.0, None, ALU.add)
            ask(d)
            then(d, d.tensor_scalar(u, u, 1.0, None, ALU.subtract))
            then(d, d.tensor_scalar(t, u, 0.0, None, ALU.is_equal))
            d.tensor_tensor(u, u, t, ALU.add)
            then(d, d.tensor_tensor(o_, o_, t, ALU.add))
            then(d, d.reciprocal(t, u))
            then(d, d.scalar_tensor_tensor(o_, o_, 0.5, t, ALU.mult, ALU.mult))
            then(d, d.tensor_tensor(o_, o_, y, ALU.mult))

        S1, S2, XN, MN, ATH, Z, TH, R, Q, GAM, GR, GM1, T1, T2, T3 = (cs(k) for k in range(15))

        def mobius_dve(d):
            root(d, S1)
            root(d, S2)
            artanh(d, ATH, XN, T1, T2, T3)
            then(d, d.reciprocal(T1, XN))
            then(d, d.tensor_tensor(T1, T1, MN, ALU.mult))
            d.tensor_tensor(Z, T1, ATH, ALU.mult)
            ask(d)
            then(d, d.reciprocal(T1, MN))
            d.tensor_tensor(R, TH, T1, ALU.mult)
            then(d, d.tensor_scalar(T2, MN, EPS, None, ALU.is_gt))
            then(d, d.tensor_tensor(R, R, T2, ALU.mult))
            then(d, d.tensor_tensor(Q, R, R, ALU.mult))
            then(d, d.tensor_tensor(Q, Q, S2, ALU.mult))
            then(d, d.tensor_scalar(Q, Q, -1.0, 1.0, ALU.mult, ALU.add))
            then(d, d.reciprocal(T1, Q))
            then(d, d.tensor_scalar(GAM, T1, 2.0, 1e-15, ALU.mult, ALU.max))
            d.tensor_tensor(GR, GAM, R, ALU.mult)
            then(d, d.tensor_scalar(GM1, GAM, 1.0, None, ALU.subtract))

        def mobius_act(a):
            answer(a, XN, S1, ACT.Sqrt)
            answer(a, MN, S2, ACT.Sqrt)
            answer(a, ATH, T2, ACT.Ln)
            answer(a, TH, Z, ACT.Tanh)

        nom, nom_end = arena(0, NB, DY)
        yr, o = arena(nom_end, NB, DYP)
        ad2, o = arena(o, N)
        at2, o = arena(o, 2, CH)
        assert o <= WORK, o
        M = {n: sem("gm_" + n) for n in ("y", "adj", "adj_used", "t", "tc", "nom", "nomc", "alpha")}

        def gm_sp(e):
            e.dma_start(yr, ty_r).then_inc(M["y"], 16)
            with e.Fori(0, NB) as i:
                e.wait_ge(M["t"], NCH * (i + 1))
                e.wait_ge(M["alpha"], i + 1)
                e.dma_start(ad2, adj[bass.ds(i * P, P), :]).then_inc(M["adj"], 16)

        def gm_pe(t):
            t.sem_inc(M["t"], NCH)
            t.wait_ge(M["y"], 16)
            with t.Fori(0, NB) as i:
                t.wait_ge(M["adj"], 16 * (i + 1))
                t.wait_ge(M["nomc"], i + 1)

                def add_chunk(c):
                    t.wait_ge(M["tc"], NCH * i + c + 1)
                    for q in range(TPC):
                        n = c * TPC + q
                        last = t.matmul(bank[5][:, 0:DY], at2[:, c % 2, q * P:(q + 1) * P], yr[:, n, 0:DY],
                                        start=(n == 0), stop=(n == NB - 1))
                    return last

                for c in range(NCH):
                    for q in range(TPC):
                        n = c * TPC + q
                        last = t.transpose(bank[3 + c % 2][:, q * P:(q + 1) * P], ad2[:, n * P:(n + 1) * P],
                                           ident[:, :])
                    last.then_inc(M["t"], 1)
                    if c:
                        add_chunk(c - 1)
                add_chunk(NCH - 1).then_inc(M["nom"], 1)

        def gm_act(a):
            a.sem_inc(M["nomc"], 1)
            with a.Fori(0, NB) as i:
                for c in range(NCH):
                    a.wait_ge(M["t"], NCH * (i + 1) + c + 1)
                    a.activation(at2[:, c % 2, :], bank[3 + c % 2][:, :], ACT.Copy).then_inc(M["tc"], 1)
                a.wait_ge(M["nom"], i + 1)
                a.activation(nom[:, bass.ds(i, 1), :], bank[5][:, 0:DY], ACT.Copy)
                a.activation(fs[:, 0, :], bank[5][:, 0:D], ACT.Square, accum_out=S0[:, bass.ds(i, 1)])
                a.drain().then_inc(M["nomc"], 1)

        def gm_dve(d):
            d.sem_inc(M["alpha"], 1)
            with d.Fori(0, NB) as i:
                d.wait_ge(M["adj"], 16 * (i + 1))
                d.tensor_reduce(alpha[:, bass.ds(i, 1)], ad2, AX, ALU.add).then_inc(M["alpha"], 1)

        assert nom_end <= WORK
        gt2, o = arena(nom_end, 2 * GT, DYP)
        gt2 = gt2.rearrange("p (k n) d -> p k n d", k=2)
        otf, o = arena(o, 2 * TILES, P)
        otf = otf.rearrange("p (k q) n -> p k q n", k=2)
        iow2, o = arena(o, EW, dt=F16)
        idb2, o = arena(o, P, dt=BF16)
        mm2, o = arena(o, 2, EW, dt=BF16)
        mm1, o = arena(o, EW, dt=BF16)
        ix2f, o = arena(o, 2, GT)
        se2, o = arena(o, 2, 2 * GB)
        assert o <= WORK, o
        ix2 = ix2f.bitcast(I32)
        F = {n: sem("fm_" + n) for n in (
            "const",
            "idx",
            "m",
            "t",
            "tc",
            "nom",
            "nomc")}
        F["gat"] = [[sem(f"fm_gat{k}{b}") for b in range(GB)] for k in range(2)]

        def fm_pool(p):
            p.iota(iow2, pattern=[[1, EW]], base=0, channel_multiplier=0, allow_small_or_imprecise_dtypes=True)
            p.tensor_copy(idb2, ident[:, :])
            p.drain().then_inc(F["const"], 1)
            with p.Fori(0, NG // 2) as j:
                for k in (0, 1):
                    g = 2 * j + k
                    p.wait_ge(F["idx"], g + 1)
                    p.wait_ge(F["nom"], GB * g + GB)
                    p.tensor_tensor(pdum[:, :], eps_t[:, :], eps_t[:, :], ALU.add)
                    p.drain()
                    for n in range(GT):
                        p.indirect_dma_start(gt2[:, k, n, :], None, table_y,
                                             bass.IndirectOffsetOnAxis(ix2[:, k, n:n + 1], 0)) \
                            .then_inc(F["gat"][k][n // TILES], 16)

        def fm_dve(d):
            d.sem_inc(F["m"], 2)
            d.wait_ge(F["const"], 1)
            with d.Fori(0, NG // 2) as j:
                for k in (0, 1):
                    g = 2 * j + k
                    d.wait_ge(F["nom"], GB * g + GB)
                    d.tensor_copy(ix2[:, k, :], idx[:, bass.ds(g * GT, GT)])
                    d.tensor_copy(se2[:, k, 0:GB], first_e[:, grp(g)])
                    d.tensor_copy(se2[:, k, GB:2 * GB], last_e[:, grp(g)])
                    d.drain().then_inc(F["idx"], 1)
                    for b in range(GB):
                        d.wait_ge(F["t"], GB * g + b + 1)
                        then(d, d.tensor_scalar(mm1, iow2, se2[:, k, GB + b:GB + b + 1], None, ALU.is_lt))
                        d.scalar_tensor_tensor(mm2[:, b % 2, :], iow2, se2[:, k, b:b + 1], mm1, ALU.is_ge, ALU.mult)
                        d.drain().then_inc(F["m"], 1)

        def fm_pe(t):
            t.sem_inc(F["t"], 2)
            t.sem_inc(F["nom"], 2 * GB)
            t.wait_ge(F["const"], 1)
            with t.Fori(0, NG // 2) as j:
                for k in (0, 1):
                    g = 2 * j + k
                    for b in range(GB):
                        t.wait_ge(F["m"], GB * g + b + 3)
                        t.wait_ge(F["tc"], GB * g + b + 1)
                        tb = bank[6 + b % 2][:, :].bitcast(BF16)
                        for q in range(TILES):
                            last = t.transpose(tb[:, q * P:(q + 1) * P], mm2[:, b % 2, q * P:(q + 1) * P], idb2)
                        last.then_inc(F["t"], 1)
                        t.wait_ge(F["tc"], GB * g + b + 3)
                        t.wait_ge(F["gat"][k][b], 8 * TILES * (g - k) + 16 * TILES)
                        t.wait_ge(F["nomc"], GB * g + b + 1)
                        for q in range(TILES):
                            last = t.matmul(bank[4 + b % 2][:, 0:DY], otf[:, b % 2, q, :],
                                            gt2[:, k, b * TILES + q, 0:DY], start=(q == 0), stop=(q == TILES - 1))
                        last.then_inc(F["nom"], 1)

        def fm_act(a):
            a.sem_inc(F["tc"], 2)
            a.sem_inc(F["nomc"], 2)
            with a.Fori(0, NG // 2) as j:
                for k in (0, 1):
                    g = 2 * j + k
                    for b in range(GB):
                        a.wait_ge(F["t"], GB * g + b + 3)
                        a.wait_ge(F["nom"], GB * g + 2 * GB + b - 1)
                        a.activation(otf[:, b % 2, :, :],
                                     bank[6 + b % 2][:, :].bitcast(BF16)[:, 0:EW].rearrange("p (q n) -> p q n", q=TILES),
                                     ACT.Copy).then_inc(F["tc"], 1)
                        a.wait_ge(F["nom"], GB * g + 2 * GB + b + 1)
                        a.activation(nom[:, at(g * GB + b), :], bank[4 + b % 2][:, 0:DY], ACT.Copy)
                        a.activation(fs[:, b % 2, :], bank[4 + b % 2][:, 0:D], ACT.Square,
                                     accum_out=S0[:, at(g * GB + b)])
                        a.drain().then_inc(F["nomc"], 1)

        S0, DN, RD, S4, WW, NN, TA, SS1, FF, S5, F3, U1, U2, U3, U4 = (cs(k) for k in range(15))
        den = nom[:, :, D]

        def midpoint_dve(d):
            then(d, d.tensor_scalar(U1, den, 0.0, None, ALU.is_ge))
            then(d, d.tensor_scalar(U1, U1, 2.0, -1.0, ALU.mult, ALU.add))
            then(d, d.tensor_tensor(DN, den, U1, ALU.mult))
            then(d, d.scalar_tensor_tensor(DN, DN, EPS, U1, ALU.max, ALU.mult))
            then(d, d.reciprocal(RD, DN))
            then(d, d.tensor_tensor(S4, S0, RD, ALU.mult))
            then(d, d.tensor_tensor(S4, S4, RD, ALU.mult))
            then(d, d.tensor_scalar(U1, S4, -1.0, 1.0, ALU.mult, ALU.add))
            d.tensor_scalar(U1, U1, EPS, None, ALU.max)
            ask(d)
            then(d, d.tensor_scalar(U2, U2, 1.0, None, ALU.add))
            then(d, d.reciprocal(WW, U2))
            then(d, d.tensor_tensor(U4, WW, WW, ALU.mult))
            then(d, d.tensor_tensor(U4, U4, S4, ALU.mult))
            then(d, d.tensor_copy(U1, U4))
            root(d, U1)
            artanh(d, TA, NN, U1, U2, U3)
            d.tensor_tensor(TA, TA, alpha[:, :], ALU.mult)
            ask(d)
            then(d, d.reciprocal(U1, NN))
            then(d, d.tensor_tensor(SS1, TA, U1, ALU.mult))
            then(d, d.tensor_tensor(U4, U4, SS1, ALU.mult))
            then(d, d.tensor_tensor(U4, U4, SS1, ALU.mult))
            root(d, U4)
            artanh(d, TA, NN, U1, U2, U3)
            then(d, d.reciprocal(U1, NN))
            then(d, d.tensor_tensor(FF, TA, U1, ALU.mult))
            then(d, d.tensor_tensor(FF, FF, SS1, ALU.mult))
            then(d, d.tensor_tensor(FF, FF, WW, ALU.mult))
            then(d, d.tensor_tensor(FF, FF, RD, ALU.mult))

        def midpoint_act(a):
            answer(a, U2, U1, ACT.Sqrt)
            answer(a, NN, U1, ACT.Sqrt)
            answer(a, TA, U2, ACT.Ln)
            answer(a, TA, TA, ACT.Tanh)
            answer(a, NN, U4, ACT.Sqrt)
            answer(a, TA, U2, ACT.Ln)

        def expmap_dve(d):
            root(d, S5)
            ask(d)
            then(d, d.reciprocal(U1, NN))
            then(d, d.tensor_tensor(F3, TA, U1, ALU.mult))

        def expmap_act(a):
            answer(a, NN, S5, ACT.Sqrt)
            answer(a, TA, NN, ACT.Tanh)
        s_u = sem("s_u")
        s_us = sem("s_us")
        s_o = sem("s_o")
        s_out = sem("s_out")

        block = ctx.enter_context(nc.Block())

        @block.sync
        def _(e):
            e.dma_start(ew, edge_w.rearrange("(c p) d -> p c d", p=P)).then_inc(s_w, 16)
            e.dma_start(nw, node_w.rearrange("(c p) d -> p (c d)", p=P), allow_slow_non_contiguous=True).then_inc(s_w, 16)
            e.dma_start(w0[:, :, :], weight.rearrange("(c p) d -> p c d", p=P)).then_inc(s_w, 16)
            e.dma_start(w1[:, :, :], W1.rearrange("(c p) d -> p c d", p=P)).then_inc(s_w, 16)
            e.dma_start(bias_bc[:, :], bias.rearrange("(a d) -> a d", a=1).broadcast_to([P, D])).then_inc(s_w, 16)

            def load(g, k):
                e.wait_ge(f0.x_used, g + 1)
                e.dma_start(xs[:, k, :, :], x_r[:, grp(g), :]).then_inc(f0.x_in[k], 16)

            def store(g, k):
                e.wait_ge(f0.h, GB * (g + 1))
                e.dma_start(th_r[:, grp(g), :], hs[:, k, :, :]).then_inc(s_th, 16)
                e.wait_ge(s_th, 16 * (g + 1))
                e.sem_inc(s_stored, 1)
            e.sem_inc(s_stored, 2)
            for n in range(2):
                for h in range(UNITS):
                    e.dma_start(adu[:, n, h, :], adj[n * P:(n + 1) * P, h * UW:(h + 1) * UW]).then_inc(L["adj"][n][h], 16)
            load(0, 0)
            skewed(e, lambda g, k: load(g + 1, 1 - k) if not isinstance(g, int) or g + 1 < NG else None, store)
            barrier(e)
            fast_load(e)
            barrier(e)
            general_if(e, ga_sp)
            barrier(e)

            def store_y(g, k):
                e.wait_ge(s_ys, g + 1)
                e.dma_start(ty_r[:, grp(g), :], ys[:, k, :, :]).then_inc(s_tyo[k], 16)
            for g in range(NG):
                store_y(g, g % 2)
            for k in (0, 1):
                e.wait_ge(s_tyo[k], 16 * NG // 2)
            barrier(e)
            general_if(e, gm_sp)
            barrier(e)
            for g in range(NG):
                e.wait_ge(s_o, GB * (g + 1))
                e.dma_start(out_r[:, grp(g), :], x1[:, grp(g), :]).then_inc(s_out, 16)
            e.wait_ge(s_out, 16 * NG)

        @block.gpsimd
        def _(p):
            p.memset(ident[:, :], 0.0)
            p.memset(eps_t[:, :], LN_EPS)
            p.drain()
            p.affine_select(out=ident[:, :], in_=ident[:, :], compare_op=ALU.not_equal, fill=1.0, base=0,
                            pattern=[[-1, P]], channel_multiplier=1)
            p.drain().then_inc(s_ident, 1)
            fast_constants(p)

            def split(g, k):
                for b in range(GB):
                    blk = at(g * GB + b)
                    p.wait_ge(s_rest, GB * g + b + 1)
                    p.tensor_copy(gx_b[:, blk, D:2 * D], res[:, k, b, :])
                    p.drain()
                    p.tensor_tensor(gx_b[:, blk, 2 * D:3 * D], res[:, k, b, :], gx_b[:, blk, D:2 * D],
                                    ALU.subtract)
                p.drain().then_inc(s_restfree, 1)
            p.sem_inc(s_restfree, 2)
            with p.Fori(0, NG // 2) as j:
                split(2 * j, 0)
                split(2 * j + 1, 1)
            p.wait_ge(s_red, 1)
            p.partition_all_reduce(cs(1)[:, 0:1], cs(0)[:, 0:1], P, RMAX)
            p.drain().then_inc(s_all, 1)
            p.wait_ge(s_exp, 1)
            p.partition_all_reduce(cs(1)[:, 2:3], cs(0)[:, 2:3], P, RADD)
            p.drain().then_inc(s_all, 1)
            barrier(p)
            fast_pool(p)
            fast_flag(p)
            barrier(p)
            general_if(p)
            barrier(p)
            p.memset(ys, 0.0)
            p.drain().then_inc(s_ysz, 1)
            barrier(p)
            general_if(p, None, fm_pool)
            barrier(p)

        @block.scalar
        def _(a):
            a.sem_inc(f0.x_used, 2)
            a.wait_ge(s_ident, 1)

            def norm(g, k):
                a.wait_ge(f0.var, g + 1)
                a.activation(std[:, :], mv[:, :, 1], ACT.Sqrt, bias=eps_t[:, 0:1])
                a.drain().then_inc(f0.sqrt, 1)
                a.wait_ge(f0.rstd, g + 1)
                a.wait_ge(f0.t, GB * (g + 1))
                a.wait_ge(s_stored, g + 1)
                for b in range(GB):
                    a.activation(hs[:, k, b, :], xs[:, k, b, :], ACT.Relu, bias=nmr[:, b:b + 1],
                                 scale=rstd[:, b:b + 1]).then_inc(f0.h, 1)
                a.drain().then_inc(f0.x_used, 1)

            def hi(g, k):
                for b in range(GB):
                    a.wait_ge(f0.prod, GB * (g + 2) + b + 1)
                    a.activation(gx_b[:, at(g * GB + b), 0:D], bank[2 + b][:, 0:D], ACT.Copy).then_inc(s_hi, 1)
            skewed(a, norm, hi)
            a.wait_ge(s_negmax, 1)
            a.activation(natt[:, :], logit[:, :], ACT.Exp, bias=cs(1)[:, 1:2], accum_out=cs(0)[:, 2:3])
            a.drain().then_inc(s_exp, 1)
            barrier(a)
            fast_act(a)
            barrier(a)
            general_if(a, ga_act)
            barrier(a)

            def norm1(g, k):
                front_norm(a, f1, x1[:, grp(g), :], g, k)
                a.wait_ge(f1.h, GB * (g + 1))
                for b in range(GB):
                    a.activation(fs[:, 0, :], hs[:, k, b, :], ACT.Square, accum_out=S1[:, at(g * GB + b)])
                    a.drain()

            def mx_out(g, k):
                for b in range(GB):
                    a.wait_ge(f1.prod, GB * (g + 2) + b + 1)
                    a.activation(mx[:, at(g * GB + b), :], bank[2 + b][:, 0:D], ACT.Copy)
                    a.activation(fs[:, 1, :], bank[2 + b][:, 0:D], ACT.Square, accum_out=S2[:, at(g * GB + b)])
                    a.drain()
                a.sem_inc(f1.prod_used, 1)
            a.sem_inc(f1.prod_used, 1)
            skewed(a, norm1, mx_out)
            a.drain().then_inc(s_sq, 1)
            mobius_act(a)
            a.wait_ge(s_gm, 1)
            a.wait_ge(s_ysz, 1)
            for g in range(NG):
                if g >= 2:
                    a.wait_ge(s_tyo[g % 2], 16 * (g // 2))
                for b in range(GB):
                    n = g * GB + b
                    a.activation(ys[:, g % 2, b, 0:D], mx[:, n, :], ACT.Copy, scale=GR[:, n:n + 1])
                    a.activation(ys[:, g % 2, b, D:DY], GM1[:, n:n + 1], ACT.Copy)
                a.drain().then_inc(s_ys, 1)
            barrier(a)
            general_if(a, gm_act, fm_act)
            barrier(a)
            midpoint_act(a)
            a.wait_ge(s_u, 1)
            for n in range(NB):
                a.activation(nom[:, n, 0:D], nom[:, n, 0:D], ACT.Relu, scale=FF[:, n:n + 1])
                a.drain()
                a.activation(fs[:, 0, :], nom[:, n, 0:D], ACT.Square, accum_out=S5[:, n:n + 1])
            a.drain().then_inc(s_us, 1)
            expmap_act(a)

        @block.tensor
        def _(t):
            for f in (f0, f1):
                t.sem_inc(f.t, 2 * GB)
                t.sem_inc(f.prod, 2 * GB)
            t.wait_ge(s_ident, 1)
            t.wait_ge(s_w, 80)
            for r in range(KD):
                for c in range(KD):
                    last = t.transpose(bank[6][:, (c * KD + r) * P:(c * KD + r + 1) * P],
                                       ew[:, r, c * P:(c + 1) * P], ident[:, :])
            last.then_inc(s_ewT, 1)
            t.wait_ge(s_ewTc, 1)
            for r in range(KD):
                for c in range(KD):
                    last = t.matmul(bank[7][:, r * D:(r + 1) * D], ewT[:, c, r * P:(r + 1) * P], ewT[:, c, :],
                                    start=(c == 0), stop=(c == KD - 1))
            last.then_inc(s_eet, 1)
            t.wait_ge(s_eet, 2)
            skewed(t, lambda g, k: front_transpose(t, f0, g, k),
                   lambda g, k: front_product(t, f0, rhs_g, DY, g, k), b_first=True)
            barrier(t)
            fast_pe(t)
            barrier(t)
            general_if(t, ga_pe)
            barrier(t)
            skewed(t, lambda g, k: front_transpose(t, f1, g, k),
                   lambda g, k: front_product(t, f1, w1, D, g, k), b_first=True)
            barrier(t)
            general_if(t, gm_pe, fm_pe)
            barrier(t)

        @block.vector
        def _(d):
            d.wait_ge(s_ewT, 1)
            d.tensor_copy(ewT.rearrange("p a b -> p (a b)"), bank[6][:, :])
            d.drain().then_inc(s_ewTc, 1)
            d.wait_ge(s_eet, 1)
            d.tensor_copy(rhs_g[:, :, 0:D], bank[7][:, :].rearrange("p (a b) -> p a b", a=KD))
            d.wait_ge(s_w, 80)
            d.tensor_copy(rhs_g[:, :, D], nw)
            d.drain().then_inc(s_eet, 1)
            for f in (f0, f1):
                d.sem_inc(f.hT, 1)
            d.sem_inc(f0.prod_used, 1)

            def first(g, k):
                d.wait_ge(f0.x_in[k], 8 * (g - k) + 16)
                front_stats(d, f0, xs[:, k, :, :], g)
                front_hT(d, f0, g, k)

            def rest(g, k):
                d.wait_ge(s_restfree, g + 1)
                for b in range(GB):
                    d.wait_ge(s_hi, GB * g + b + 1)
                    d.tensor_tensor(res[:, k, b, :], bank[2 + b][:, 0:D], gx_b[:, at(g * GB + b), 0:D],
                                    ALU.subtract).then_inc(s_rest, 1)
                    d.tensor_copy(logit[:, at(g * GB + b)], bank[2 + b][:, D:DY])
                d.drain().then_inc(f0.prod_used, 1)
            skewed(d, first, rest)
            d.tensor_reduce(cs(0)[:, 0:1], logit[:, :], AX, ALU.max)
            d.drain().then_inc(s_red, 1)
            d.wait_ge(s_all, 1)
            d.tensor_scalar(cs(1)[:, 1:2], cs(1)[:, 0:1], -1.0, None, ALU.mult)
            d.drain().then_inc(s_negmax, 1)
            d.wait_ge(s_all, 2)
            d.reciprocal(cs(1)[:, 3:4], cs(1)[:, 2:3])
            d.drain()
            d.tensor_scalar(natt[:, :], natt[:, :], cs(1)[:, 3:4], None, ALU.mult)
            barrier(d)
            fast_dve(d)
            barrier(d)
            general_if(d, ga_dve)
            barrier(d)

            def first1(g, k):
                front_stats(d, f1, x1[:, grp(g), :], g)
                front_hT(d, f1, g, k)
            with d.Fori(0, NG // 2) as j:
                first1(2 * j, 0)
                first1(2 * j + 1, 1)
            d.wait_ge(s_sq, 1)
            mobius_dve(d)
            d.drain().then_inc(s_gm, 1)
            barrier(d)
            general_if(d, gm_dve, fm_dve)
            barrier(d)
            midpoint_dve(d)
            d.drain().then_inc(s_u, 1)
            d.wait_ge(s_us, 1)
            expmap_dve(d)
            d.drain()
            for n in range(NB):
                d.scalar_tensor_tensor(x1[:, n, :], nom[:, n, 0:D], F3[:, n:n + 1], x1[:, n, :], ALU.mult,
                                       ALU.add).then_inc(s_o, 1)


_INS = ['x', 'adj', 'L0_gnn_weight', 'L0_gnn_bias', 'L0_gnn_node_w', 'L0_gnn_edge_w', 'L1_gnn_W']


def kernel(**inputs):
    import numpy as np
    import concourse.bacc as bacc
    from concourse.bass_utils import run_bass_kernel_spmd

    nc = bacc.Bacc("TRN2", target_bir_lowering=False, num_devices=1)
    arrays, args = {}, []
    for name in _INS:
        a = np.ascontiguousarray(inputs[name])
        arrays[f"in_{name}"] = a
        args.append(nc.dram_tensor(f"in_{name}", a.shape, mybir.dt.from_np(a.dtype), kind="ExternalInput").ap())
    out = nc.dram_tensor("out_0", inputs['x'].shape, F32, kind="ExternalOutput").ap()
    gnn_program(nc, *args, out)
    return run_bass_kernel_spmd(nc, [arrays], core_ids=[0]).results[0]["out_0"]
```

```python
from contextlib import ExitStack

import concourse.bass as bass
from concourse import mybir

P = 128
ALU = mybir.AluOpType
ACT = mybir.ActivationFunctionType
F32 = mybir.dt.float32
BF16 = mybir.dt.bfloat16
F16 = mybir.dt.float16
I32 = mybir.dt.int32
AX = mybir.AxisListType.X
RMAX = bass.bass_isa.ReduceOp.max
RADD = bass.bass_isa.ReduceOp.add

LN_EPS = 1e-5
EPS = 1e-10
CLIP = 1.0 - 1e-7
NEG_BIG = -9000000000000000.0
GB = 4
SLOTS = 16
BPW = 3
TILES = 5


def gnn_program(nc, x, adj, weight, bias, node_w, edge_w, W1, out):
    N, D = x.shape
    NB = N // P
    NG = NB // GB
    assert NG % 2 == 0 and NG >= 4
    KD = D // P
    DY = D + 1
    DYP = DY + 3
    CH = 512
    NCH = N // CH
    WORK = 30240
    P0_AT = 23500
    KEY = 256
    BITS = N // KEY
    UNITS = 2
    UW = N // UNITS
    GT = GB * TILES
    EW = TILES * P
    EXP = 127 + 8
    MASK = -(1 << 23)
    TPC = CH // P

    table_h = nc.dram_tensor("table_h", [N, D], F32, kind="Internal").ap()
    table_y = nc.dram_tensor("table_y", [N, DYP], F32, kind="Internal").ap()

    rows = lambda t: t.rearrange("(b p) d -> p b d", p=P)
    x_r, out_r, th_r, ty_r = rows(x), rows(out), rows(table_h), rows(table_y)

    with ExitStack() as ctx:
        def sb(name, shape, dt=F32):
            return ctx.enter_context(nc.sbuf_tensor(name, shape, dt))

        def sem(name):
            return ctx.enter_context(nc.semaphore(name))

        bank = [ctx.enter_context(nc.psum_tensor(f"bank{i}", [P, CH], F32)) for i in range(8)]

        ident = sb("ident", [P, P])
        rhs_g = sb("rhs_g", [P, KD, DY])
        w0 = sb("w0", [P, KD, D])
        w1 = sb("w1", [P, KD, D])
        bias_bc = sb("bias_bc", [P, D])
        eps_t = sb("eps_t", [P, 1])
        GXW = 3 * D // 2
        gx = sb("gx", [P, NB, GXW])
        gx_b = gx[:, :, :].rearrange("p b c -> p (b c)").bitcast(BF16).rearrange("p (b c) -> p b c", b=NB)
        x1 = gx[:, :, 0:D]
        logit = sb("logit", [P, NB])
        natt = sb("natt", [P, NB])
        alpha = sb("alpha", [P, NB])
        col = sb("col", [P, 24, NB])
        cs = lambda k: col[:, k, :]
        front = sb("front", [P, 3, 2 * GB * D])
        xs = front[:, 0, :].rearrange("p (k b d) -> p k b d", k=2, b=GB)
        hs = front[:, 1, :].rearrange("p (k b d) -> p k b d", k=2, b=GB)
        hT = front[:, 2, :].rearrange("p (k b c n) -> p k b c n", k=2, b=GB, c=KD)
        S1g = sb("S1g", [P, 2, GB])
        stats = sb("stats", [P, GB, 6])
        mv = sb("mv", [P, GB, 2])
        std = sb("std", [P, GB])
        rstd = sb("rstd", [P, GB])
        nmr = sb("nmr", [P, GB])
        fs = sb("fs", [P, 4, D])
        work = sb("work", [P, WORK])

        def arena(off, *shape, dt=F32):
            n = 1
            for s in shape:
                n *= s
            words = n if dt == F32 else (n + 1) // 2
            v = work[:, off:off + words]
            if dt != F32:
                v = v.bitcast(dt)
            if len(shape) == 2:
                v = v.rearrange("p (a b) -> p a b", a=shape[0])
            if len(shape) == 3:
                v = v.rearrange("p (a b c) -> p a b c", a=shape[0], b=shape[1])
            return v, off + words

        bar = sem("bar")
        bars = {}

        def barrier(eng):
            n = bars.get(eng, 0) + 1
            bars[eng] = n
            eng.drain().then_inc(bar, 1)
            eng.wait_ge(bar, 5 * n)

        def staged(eng, body):
            def step(n):
                stage = lambda d: (n - d, (n - d) % 2) if 0 <= n - d < NG else None
                body(stage(0), stage(1), stage(2), stage(3))
            for n in range(3):
                step(n)
            with eng.Fori(0, (NG - 3) // 2) as j:
                for k in (0, 1):
                    g = 2 * j + k
                    body((g + 3, 1 - k), (g + 2, k), (g + 1, 1 - k), (g, k))
            for n in range(3 + (NG - 3) // 2 * 2, NG + 3):
                step(n)

        grp = lambda g: bass.ds(g * GB, GB) if not isinstance(g, int) else slice(g * GB, g * GB + GB)
        at = lambda b, n=1: bass.ds(b, n) if not isinstance(b, int) else slice(b, b + n)

        class Front:
            def __init__(self, t):
                self.x_in = [sem(f"{t}_x_in0"), sem(f"{t}_x_in1")]
                self.x_used = sem(f"{t}_x_used")
                self.var = sem(f"{t}_var")
                self.sqrt = sem(f"{t}_sqrt")
                self.rstd = sem(f"{t}_rstd")
                self.h = sem(f"{t}_h")
                self.t = sem(f"{t}_t")
                self.hT = sem(f"{t}_hT")
                self.prod = sem(f"{t}_prod")
                self.prod_used = sem(f"{t}_prod_used")

        f0 = Front("f0")
        f1 = Front("f1")

        def front_stats(d, f, src, g):
            for b in range(GB):
                d.bn_stats(stats[:, b, :], src[:, b, :])
            d.drain()
            for b in range(GB):
                d.bn_aggr(mv[:, b, :], stats[:, b, :])
            d.drain().then_inc(f.var, 1)

        def front_scale(d, f, g):
            d.wait_ge(f.sqrt, g + 1)
            d.reciprocal(rstd[:, :], std[:, :])
            d.drain()
            d.scalar_tensor_tensor(nmr[:, :], mv[:, :, 0], -1.0, rstd[:, :], ALU.mult, ALU.mult)
            d.drain().then_inc(f.rstd, 1)

        def front_std(a, f, g):
            a.wait_ge(f.var, g + 1)
            a.activation(std[:, :], mv[:, :, 1], ACT.Sqrt, bias=eps_t[:, 0:1])
            a.drain().then_inc(f.sqrt, 1)

        def front_norm(a, f, src, g, k):
            a.wait_ge(f.rstd, g + 1)
            a.wait_ge(f.t, GB * (g + 1))
            for b in range(GB):
                a.activation(hs[:, k, b, :], src[:, b, :], ACT.Relu, bias=nmr[:, b:b + 1],
                             scale=rstd[:, b:b + 1]).then_inc(f.h, 1)

        def front_transpose(t, f, g, k):
            t.wait_ge(f.hT, g + 1)
            for b in range(GB):
                t.wait_ge(f.h, GB * g + b + 1)
                for c in range(KD):
                    last = t.transpose(bank[b // 2][:, ((b % 2) * KD + c) * P:((b % 2) * KD + c + 1) * P],
                                       hs[:, k, b, c * P:(c + 1) * P], ident[:, :])
                last.then_inc(f.t, 1)

        def front_hT(d, f, g, k):
            d.wait_ge(f.prod, GB * (g + 1))
            for j in range(GB // 2):
                d.wait_ge(f.t, GB * (g + 2) + 2 * j + 2)
                d.tensor_copy(hT[:, k, 2 * j:2 * j + 2, :, :].rearrange("p b c n -> p (b c n)"), bank[j][:, :])
            d.drain().then_inc(f.hT, 1)

        def front_product(t, f, rhs, n, g, k):
            t.wait_ge(f.hT, g + 2)
            t.wait_ge(f.prod_used, g + 1)
            for b in range(GB):
                for c in range(KD):
                    last = t.matmul(bank[2 + b][:, 0:n], hT[:, k, b, c, :], rhs[:, c, 0:n],
                                    start=(c == 0), stop=(c == KD - 1))
                last.then_inc(f.prod, 1)

        ew, o = arena(P0_AT, KD, D)
        ewT, o = arena(o, KD, D)
        res, o = arena(o, 2, GB, D)
        nw, o = arena(o, KD)

        s_go = sem("s_go")
        s_w = sem("s_w")
        s_w2 = sem("s_w2")
        s_ident = sem("s_ident")
        s_ewT = sem("s_ewT")
        s_ewTc = sem("s_ewTc")
        s_eet = sem("s_eet")
        s_hi = sem("s_hi")
        s_rest = sem("s_rest")
        s_mid = sem("s_mid")
        s_restfree = sem("s_restfree")
        s_th = [sem("s_th0"), sem("s_th1")]
        s_red = sem("s_red")
        s_all = sem("s_all")
        s_negmax = sem("s_negmax")
        s_exp = sem("s_exp")

        hn, o = arena(0, NB, D)
        hnT, o = arena(o, KD, N)
        em, o = arena(o, N)
        ad, o = arena(o, N)
        pt, o = arena(o, 2, CH)
        stg, o = arena(o, D)
        gT, o = arena(o, KD, P)
        xr, o = arena(o, D)
        ag, o = arena(o, D)
        agT, o = arena(o, KD, P)
        sc, o = arena(o, 8)
        assert o <= WORK, o
        A = {n: sem("ga_" + n) for n in (
            "hn", "staged", "stage_free", "setT", "setTc", "adj", "x", "done", "gT", "gTc", "scores",
            "masked", "max", "exp", "weights", "pt", "ptc", "agg", "aggc", "aggT", "aggTc", "proj")}

        def ga_sp(e):
            e.dma_start(hn, th_r).then_inc(A["hn"], 16)
            with e.Fori(0, NB) as i:
                e.wait_ge(A["done"], i + 1)
                e.dma_start(ad, adj[bass.ds(i * P, P), :]).then_inc(A["adj"], 16)
                e.dma_start(xr, x[bass.ds(i * P, P), :]).then_inc(A["x"], 16)
            e.wait_ge(A["done"], NB + 1)

        def ga_dve(d):
            d.sem_inc(A["done"], 1)
            d.sem_inc(A["masked"], 2)
            d.wait_ge(A["hn"], 16)
            with d.Fori(0, NB) as t:
                d.wait_ge(A["stage_free"], t + 1)
                d.tensor_copy(stg, hn[:, bass.ds(t, 1), :])
                d.drain().then_inc(A["staged"], 1)
            with d.Fori(0, NB) as i:
                d.wait_ge(A["adj"], 16 * (i + 1))
                d.tensor_scalar(em, ad, 0.0, NEG_BIG, ALU.is_le, ALU.mult)
                d.drain()
                for c in range(NCH):
                    d.wait_ge(A["scores"], NCH * i + c + 1)
                    d.tensor_tensor(em[:, c * CH:(c + 1) * CH], em[:, c * CH:(c + 1) * CH],
                                    bank[c % 2][:, :], ALU.add).then_inc(A["masked"], 1)
                d.drain()
                d.tensor_reduce(sc[:, 0:1], em, AX, ALU.max)
                d.drain()
                d.tensor_scalar(sc[:, 1:2], sc[:, 0:1], -1.0, None, ALU.mult)
                d.drain().then_inc(A["max"], 1)
                d.wait_ge(A["exp"], i + 1)
                d.tensor_tensor(em, em, ad, ALU.mult)
                d.drain().then_inc(A["weights"], 1)
                d.reciprocal(sc[:, 3:4], sc[:, 2:3])
                d.wait_ge(A["x"], 16 * (i + 1))
                d.tensor_tensor(xr, xr, bias_bc[:, :], ALU.add)
                d.drain()
                d.tensor_tensor(sc[:, 4:5], sc[:, 3:4], natt[:, bass.ds(i, 1)], ALU.mult)
                d.drain()
                d.wait_ge(A["proj"], i + 1)
                d.scalar_tensor_tensor(x1[:, bass.ds(i, 1), :], bank[7][:, 0:D], sc[:, 4:5], xr, ALU.mult, ALU.add)
                d.drain().then_inc(A["done"], 1)

        def ga_pe(t):
            t.sem_inc(A["stage_free"], 1)
            with t.Fori(0, NB) as i:
                t.wait_ge(A["staged"], i + 1)
                t.wait_ge(A["setTc"], i + 1)
                for c in range(KD):
                    last = t.transpose(bank[2][:, c * P:(c + 1) * P], stg[:, c * P:(c + 1) * P], ident[:, :])
                t.drain().then_inc(A["stage_free"], 1)
                t.sem_inc(A["setT"], 1)
            t.wait_ge(A["setTc"], NB + 1)
            with t.Fori(0, NB) as i:
                for r in range(KD):
                    for c in range(KD):
                        last = t.matmul(bank[2][:, r * P:(r + 1) * P], rhs_g[:, c, r * P:(r + 1) * P],
                                        hnT[:, c, bass.ds(i * P, P)], start=(c == 0), stop=(c == KD - 1))
                last.then_inc(A["gT"], 1)
                t.wait_ge(A["gTc"], i + 1)
                for c in range(NCH):
                    t.wait_ge(A["masked"], NCH * i + c + 1)
                    for k in range(KD):
                        last = t.matmul(bank[c % 2][:, :], gT[:, k, :], hnT[:, k, c * CH:(c + 1) * CH],
                                        start=(k == 0), stop=(k == KD - 1))
                    last.then_inc(A["scores"], 1)
                t.wait_ge(A["weights"], i + 1)

                def add_chunk(c):
                    t.wait_ge(A["ptc"], NCH * i + c + 1)
                    for q in range(TPC):
                        n = c * TPC + q
                        last = t.matmul(bank[5][:, 0:D], pt[:, c % 2, q * P:(q + 1) * P], hn[:, n, :],
                                        start=(n == 0), stop=(n == NB - 1))
                    return last

                for c in range(NCH):
                    for q in range(TPC):
                        n = c * TPC + q
                        last = t.transpose(bank[3 + c % 2][:, q * P:(q + 1) * P], em[:, n * P:(n + 1) * P],
                                           ident[:, :])
                    last.then_inc(A["pt"], 1)
                    if c:
                        add_chunk(c - 1)
                add_chunk(NCH - 1).then_inc(A["agg"], 1)
                t.wait_ge(A["aggc"], i + 1)
                for k in range(KD):
                    last = t.transpose(bank[6][:, k * P:(k + 1) * P], ag[:, k * P:(k + 1) * P], ident[:, :])
                last.then_inc(A["aggT"], 1)
                t.wait_ge(A["aggTc"], i + 1)
                for k in range(KD):
                    last = t.matmul(bank[7][:, 0:D], agT[:, k, :], w0[:, k, :], start=(k == 0), stop=(k == KD - 1))
                last.then_inc(A["proj"], 1)

        def ga_act(a):
            a.sem_inc(A["setTc"], 1)
            with a.Fori(0, NB) as t:
                a.wait_ge(A["setT"], t + 1)
                for c in range(KD):
                    a.activation(hnT[:, c, bass.ds(t * P, P)], bank[2][:, c * P:(c + 1) * P], ACT.Copy)
                a.drain().then_inc(A["setTc"], 1)
            with a.Fori(0, NB) as i:
                a.wait_ge(A["gT"], i + 1)
                a.activation(gT.rearrange("p a b -> p (a b)"), bank[2][:, 0:D], ACT.Copy).then_inc(A["gTc"], 1)
                a.wait_ge(A["max"], i + 1)
                a.activation(em, em, ACT.Exp, bias=sc[:, 1:2], accum_out=sc[:, 2:3]).then_inc(A["exp"], 1)
                for c in range(NCH):
                    a.wait_ge(A["pt"], NCH * i + c + 1)
                    a.activation(pt[:, c % 2, :], bank[3 + c % 2][:, :], ACT.Copy).then_inc(A["ptc"], 1)
                a.wait_ge(A["agg"], i + 1)
                a.activation(ag, bank[5][:, 0:D], ACT.Copy).then_inc(A["aggc"], 1)
                a.wait_ge(A["aggT"], i + 1)
                a.activation(agT.rearrange("p a b -> p (a b)"), bank[6][:, 0:D], ACT.Copy).then_inc(A["aggTc"], 1)

        adu, o = arena(0, 2, UNITS, UW)
        abf, o = arena(o, UNITS, UW, dt=BF16)
        gat, o = arena(o, 2 * GT, D)
        gat = gat.rearrange("p (k n) d -> p k n d", k=2)
        wid, o = arena(o, BITS, P, dt=BF16)
        idb, o = arena(o, P, dt=BF16)
        iokb, o = arena(o, KEY, dt=BF16)
        upper, o = arena(o, P, dt=BF16)
        iow, o = arena(o, EW, dt=F16)
        iok, o = arena(o, KEY)
        posc, o = arena(o, TILES)
        t16, o = arena(o, 2, GB, SLOTS)
        ia, o = arena(o, GB, SLOTS)
        ib, o = arena(o, GB, SLOTS)
        wf, o = arena(o, GB, SLOTS)
        cf, o = arena(o, GB, SLOTS)
        tp, o = arena(o, GB, SLOTS)
        r1, o = arena(o, GB, SLOTS)
        e48, o = arena(o, GB, BPW * SLOTS)
        s16, o = arena(o, GB, SLOTS)
        nv, o = arena(o, 2, GB)
        nvb, o = arena(o, GB, dt=BF16)
        cnt, o = arena(o, 2, GB, UNITS)
        ends, o = arena(o, 2, GB)
        vt, o = arena(o, GB, 2 * SLOTS + 2, dt=F16)
        oh, o = arena(o, 2 * GT, SLOTS)
        oh = oh.rearrange("p (k n) s -> p k n s", k=2)
        rr, o = arena(o, GT)
        jt, o = arena(o, GT, SLOTS)
        jj, o = arena(o, GT)
        ixf, o = arena(o, 2, GT)
        ee, o = arena(o, 2, GT)
        es, o = arena(o, GB, SLOTS)
        sm, o = arena(o, 6, GB)
        pr, o = arena(o, GB, SLOTS)
        e3, o = arena(o, GT, 4, dt=BF16)
        m3, o = arena(o, GB, 4, dt=BF16)
        pe_, o = arena(o, GT)
        ot, o = arena(o, GT, P, dt=BF16)
        otp, o = arena(o, GT, P)
        am1, o = arena(o, GB, EW, dt=BF16)
        assert o <= WORK, o
        xr2 = xs
        flat = front[:, :, :].rearrange("p a n -> p (a n)")
        am = flat[:, 2 * GB * D:2 * GB * D + GB * EW].bitcast(BF16).rearrange("p (k b e) -> p k b e", k=2, b=GB)
        spare = flat[:, 2 * GB * D + GB * EW:]
        key = spare[:, 0:2 * KEY].rearrange("p (a b) -> p a b", a=2)
        aT = spare[:, 2 * KEY:2 * KEY + 2 * D].rearrange("p (k c n) -> p k c n", k=2, c=KD)
        low = spare[:, 2 * KEY + 2 * D:].bitcast(BF16)
        oe = low[:, 0:GT * 3 * SLOTS].rearrange("p (n q s) -> p n q s", q=3, s=SLOTS)
        zeros = low[:, GT * 3 * SLOTS:GT * 3 * SLOTS + GB * SLOTS]
        junk = fs[:, :, :]
        idx = sb("idx", [P, NB * TILES], I32)
        first_e = sb("first_e", [P, NB])
        last_e = sb("last_e", [P, NB])
        bad = sb("bad", [P, NB])
        badc = sb("badc", [P, 2])
        ddum = sb("ddum", [P, 1])
        tab = sb("tab", [P, 1])
        flag = sb("flag", [P, 1], I32)
        t6b = bank[6][:, :].bitcast(BF16)

        L = {n: sem("fa_" + n) for n in (
            "conv",
            "pack",
            "key",
            "nv",
            "start",
            "m",
            "v",
            "idx",
            "x",
            "xb",
            "ott",
            "otc",
            "exp_g",
            "dot",
            "ohe",
            "es",
            "smax",
            "m3",
            "pexp",
            "mx",
            "den",
            "less",
            "otp",
            "otp_act",
            "agg",
            "aggc",
            "proj",
            "x1",
            "flag1")}
        L["adj"] = [[sem(f"fa_adj{n}{h}") for h in range(UNITS)] for n in range(2)]
        L["gat"] = [[sem(f"fa_gat{k}{b}") for b in range(GB)] for k in range(2)]

        def fast_constants(p):
            p.iota(iow, pattern=[[1, EW]], base=0, channel_multiplier=0, allow_small_or_imprecise_dtypes=True)
            p.iota(iok, pattern=[[1, KEY]], base=0, channel_multiplier=0, allow_small_or_imprecise_dtypes=True)
            p.drain()
            p.iota(posc, pattern=[[P, TILES]], base=0, channel_multiplier=1, allow_small_or_imprecise_dtypes=True)
            p.memset(wid, 0.0)
            p.tensor_copy(idb, ident[:, :])
            p.tensor_copy(iokb, iok)
            p.memset(upper, 1.0)
            p.memset(bad[:, :], 0.0)
            p.drain()
            for m in range(BITS):
                p.affine_select(out=wid[:, m, :], in_=wid[:, m, :], compare_op=ALU.not_equal, fill=float(KEY << m),
                                base=0, pattern=[[-1, P]], channel_multiplier=1)
            p.affine_select(out=upper, in_=upper, compare_op=ALU.is_gt, fill=0.0, base=0, pattern=[[1, P]],
                            channel_multiplier=-1)
            p.drain()

        def fast_load(e):
            with e.Fori(0, (NB - 2) // 2) as j:
                for n in range(2):
                    for h in range(UNITS):
                        e.wait_ge(L["conv"], 2 * UNITS * j + UNITS * n + h + 1)
                        e.dma_start(adu[:, n, h, :], adj[bass.ds((2 * j + 2 + n) * P, P), h * UW:(h + 1) * UW]) \
                            .then_inc(L["adj"][n][h], 16)

        def fast_act(a):
            a.sem_inc(L["otc"], 1)

            def body(wd, ls, at_, ag_):
                def conv(u, group):
                    if group:
                        g, k = group
                        b, h = u // UNITS, u % UNITS
                        if u == 0 and not (isinstance(g, int) and g < 2):
                            a.wait_ge(L["nv"], g - 1)
                        a.wait_ge(L["adj"][b % 2][h], 16 * (2 * g + b // 2 + 1))
                        a.wait_ge(L["pack"], UNITS * GB * g + UNITS * b + h + 1)
                        a.activation(abf[:, h, :], adu[:, b % 2, h, :], ACT.Copy,
                                     accum_out=cnt[:, k, b, h:h + 1]).then_inc(L["conv"], 1)

                ahead = (wd[0] + 1, 1 - wd[1]) if wd and not (isinstance(wd[0], int) and wd[0] + 1 >= NG) else None
                def ott(b):
                    if at_:
                        g, k = at_
                        if b == 0:
                            a.wait_ge(L["otp"], g + 1)
                        a.wait_ge(L["ott"], GB * g + b + 1)
                        a.activation(ot[:, b * TILES:(b + 1) * TILES, :],
                                     t6b[:, 0:EW].rearrange("p (q n) -> p q n", q=TILES),
                                     ACT.Copy).then_inc(L["otc"], 1)

                def aggregate(b):
                    if ag_:
                        g, k = ag_
                        a.wait_ge(L["agg"], GB * g + b + 2 * GB + 1)
                        a.wait_ge(L["proj"], GB * g + b + 1)
                        a.activation(aT[:, b % 2, :, :].rearrange("p c n -> p (c n)"), bank[4 + b % 2][:, 0:D],
                                     ACT.Copy).then_inc(L["aggc"], 1)

                if ls and not at_:
                    a.wait_ge(s_negmax, 1)
                    a.activation(natt[:, :], logit[:, :], ACT.Exp, bias=cs(1)[:, 1:2], accum_out=cs(0)[:, 2:3])
                    a.drain().then_inc(s_exp, 1)
                for b in (0, 1):
                    ott(2 * b)
                    ott(2 * b + 1)
                    aggregate(b)
                for u in range(2 if ls else 0, UNITS * GB):
                    conv(u, wd)
                for b in (2, 3):
                    aggregate(b)
                if at_:
                    g, k = at_
                    a.wait_ge(L["smax"], g + 1)
                    for b in range(GB):
                        a.activation(pr[:, b, :], es[:, b, :], ACT.Exp, bias=sm[:, 1, b:b + 1],
                                     accum_out=sm[:, 2, b:b + 1])
                    a.drain().then_inc(L["den"], 1)
                conv(0, ahead)
                conv(1, ahead)
                if at_:
                    a.wait_ge(L["less"], g + 1)
                    a.activation(pe_, ee[:, 1, :], ACT.Exp).then_inc(L["pexp"], 1)
                    a.wait_ge(L["agg"], GB * g + 2 * GB)
                    a.wait_ge(L["pexp"], g + 1)
                    for n in range(BY_DVE, GT):
                        last = a.activation(otp[:, n, :], ot[:, n, :], ACT.Copy, scale=pe_[:, n:n + 1])
                    last.then_inc(L["otp_act"], 1)
            staged(a, body)

        def fast_pool(p):
            def body(wd, ls, at_, ag_):
                if ls:
                    g, k = ls
                    p.wait_ge(L["agg"], GB * g + 2)
                    p.wait_ge(L["idx"], g + 1)
                    p.sem_inc(s_go, 1)
                    for n in range(GT):
                        if n == GT // 2:
                            p.wait_ge(L["agg"], GB * g + GB)
                            p.sem_inc(s_go, 1)
                        p.indirect_dma_start(gat[:, k, n, :], None, table_h,
                                             bass.IndirectOffsetOnAxis(ix[:, k, n:n + 1], 0)) \
                            .then_inc(L["gat"][k][n // TILES], 16)
                    p.wait_ge(L["x1"], GB * g + GB)
                    p.dma_start(xr2[:, k, :, :], x_r[:, grp(g), :]).then_inc(L["x"], 16)
                    p.wait_ge(L["x"], 16 * (g + 1))
                    for b in range(GB):
                        p.tensor_tensor(xr2[:, k, b, :], xr2[:, k, b, :], bias_bc[:, :], ALU.add)
                    p.drain().then_inc(L["xb"], 1)
            staged(p, body)

        ix = ixf.bitcast(I32)

        def fast_flag(p):
            p.wait_ge(L["flag1"], 1)
            p.partition_all_reduce(badc[:, 1:2], badc[:, 0:1], P, RMAX)
            p.drain()
            p.tensor_copy(flag[:, :], badc[:, 1:2])
            p.drain()

        def general_if(eng, general=None, fast=None):
            f = eng.value_load(flag[0:1, 0:1], min_val=0, max_val=1)
            with eng.If(f > 0):
                if general:
                    general(eng)
                eng.nop()
            with eng.Else():
                if fast:
                    fast(eng)
                eng.nop()

        BY_DVE = GT - 10
        EB = (3, 4, 5)

        def fast_pe(t):
            t.sem_inc(L["pack"], UNITS)
            t.sem_inc(L["agg"], 2 * GB)
            t.sem_inc(L["proj"], 2)

            def body(wd, ls, at_, ag_):
                def pack(u):
                    if wd:
                        g, k = wd
                        b, h = u // UNITS, u % UNITS
                        if h == 0:
                            t.wait_ge(L["key"], GB * g + b + 1)
                            t.matmul(bank[b % 2][:, 0:KEY], idb, iokb, start=True, stop=False)
                        t.wait_ge(L["conv"], UNITS * GB * g + UNITS * b + h + 1)
                        for m in range(BITS // UNITS):
                            mm = h * BITS // UNITS + m
                            last = t.matmul(bank[b % 2][:, 0:KEY], wid[:, mm, :], abf[:, h, m * KEY:(m + 1) * KEY],
                                            start=False, stop=(mm == BITS - 1))
                        last.then_inc(L["pack"], 1)

                def proj(b):
                    if not ag_:
                        return
                    g, k = ag_
                    t.wait_ge(L["aggc"], GB * g + b + 1)
                    if b == 0:
                        t.wait_ge(L["x1"], GB * g + 2 * GB)
                    if b == 2 and at_:
                        t.wait_ge(L["otc"], GB * at_[0] + GB + 1)
                    for c in range(KD):
                        last = t.matmul(bank[7 - b // 2][:, b % 2 * D:(b % 2 + 1) * D], aT[:, b % 2, c, :], w0[:, c, :],
                                        start=(c == 0), stop=(c == KD - 1))
                    last.then_inc(L["proj"], 1)

                def ott(b):
                    if at_:
                        g, k = at_
                        if b == 0 and not ag_:
                            t.wait_ge(s_restfree, NG + 2)
                        if b == 0:
                            t.wait_ge(L["x1"], GB * g + GB)
                        t.wait_ge(L["otc"], GB * g + b + 1)
                        for q in range(TILES):
                            last = t.transpose(t6b[:, q * P:(q + 1) * P], am[:, k, b, q * P:(q + 1) * P], idb)
                        last.then_inc(L["ott"], 1)

                def aggregate(b, c):
                    if ag_:
                        g, k = ag_
                        if b == 0:
                            t.wait_ge(L["otp"], g + 2)
                        if (b + 1) * TILES > BY_DVE:
                            t.wait_ge(L["otp_act"], g + 1)
                        if b == 2 and at_:
                            t.wait_ge(L["dot"], GT * at_[0] + GT)
                        elif b >= 2:
                            t.wait_ge(L["aggc"], GB * g + b - 1)
                        for q in range(TILES):
                            n = b * TILES + q
                            last = t.matmul(bank[4 + b % 2][:, c * P:(c + 1) * P],
                                            gat[:, k, n, c * P:(c + 1) * P], otp[:, n, :],
                                            start=(q == 0), stop=(q == TILES - 1))
                        if c == KD - 1:
                            last.then_inc(L["agg"], 1)

                if ls:
                    t.wait_ge(L["nv"], ls[0] + 1)
                    t.matmul(bank[2][:, 0:GB], upper, nvb, start=True, stop=True).then_inc(L["start"], 1)
                if ag_ and not (isinstance(ag_[0], int) and ag_[0] == 0):
                    t.wait_ge(L["aggc"], GB * ag_[0])
                for b in range(GB):
                    ott(b)
                    if b < GB - 1:
                        aggregate(b // 2, b % 2)
                if not at_:
                    pack(0)
                    pack(1)
                if ls:
                    g, k = ls
                    for b in range(GB):
                        t.wait_ge(L["m"], GB * g + b + 1)
                        for q in range(TILES):
                            last = t.matmul(bank[2 + b // 2][:, ((b % 2) * TILES + q) * 33:
                                                             ((b % 2) * TILES + q) * 33 + 33],
                                            am[:, k, b, q * P:(q + 1) * P], vt[:, b, 0:33], start=True, stop=True)
                        if b % 2:
                            last.then_inc(L["v"], 1)
                aggregate(1, 1)
                proj(0)
                if at_:
                    pack(0)
                proj(1)
                if at_:
                    pack(1)
                if at_ and ag_:
                    t.wait_ge(L["aggc"], GB * ag_[0] + 2)

                def exp_g(first, last_):
                    if at_:
                        g, k = at_
                        for p in range(first, last_):
                            if p >= 3:
                                t.wait_ge(L["dot"], GT * g + 2 * (p - 3) + 2)
                            elif p == 0 and ls:
                                t.wait_ge(L["idx"], ls[0] + 1)
                            for n in (2 * p, 2 * p + 1):
                                b, q = n // TILES, n % TILES
                                for c in range(3):
                                    last = t.matmul(bank[EB[p % 3]][:, n % 2 * D:(n % 2 + 1) * D],
                                                    am[:, k, b, q * P:(q + 1) * P],
                                                    gx_b[:, at(g * GB + b), c * D:(c + 1) * D],
                                                    start=(c == 0), stop=(c == 2))
                            last.then_inc(L["exp_g"], 1)
                exp_g(0, GT // 4)
                pack(2)
                pack(3)
                exp_g(GT // 4, GT // 4 + 2)
                pack(4)
                pack(5)
                exp_g(GT // 4 + 2, GT // 2)
                pack(6)
                pack(7)
                if at_:
                    g, k = at_
                    t.wait_ge(L["ohe"], g + 1)
                    t.wait_ge(L["otc"], GB * g + GB + 1)
                    t.matmul(bank[2][:, 0:GB * SLOTS], ot[:, 0, :], zeros, start=True, stop=False)
                    for q in range(TILES):
                        for b in range(GB):
                            n = b * TILES + q
                            for v in range(3):
                                last = t.matmul(bank[2][:, b * SLOTS:(b + 1) * SLOTS], ot[:, n, :], oe[:, n, v, :],
                                                start=False, stop=(q == TILES - 1 and b == GB - 1 and v == 2))
                    last.then_inc(L["es"], 1)
                for b in (2, 3):
                    for c in range(KD):
                        aggregate(b, c)
                proj(2)
                proj(3)
                if at_:
                    t.wait_ge(L["m3"], g + 1)
                    for n in range(GT):
                        last = t.matmul(bank[3][:, n * 4:n * 4 + 3], am[:, k, n // TILES, n % TILES * P:
                                                                        (n % TILES + 1) * P],
                                        m3[:, n // TILES, 0:3], start=True, stop=True)
                    last.then_inc(L["mx"], 1)
            staged(t, body)

        def fast_dve(d):
            d.memset(zeros, 0.0)
            d.drain().then_inc(L["key"], 2)
            d.sem_inc(L["otp"], 1)
            d.sem_inc(L["x1"], 2 * GB)
            bc = lambda v, shape, axis: v.unsqueeze(axis).broadcast_to(shape)

            def keys(g, k, pair):
                bs = (2 * pair, 2 * pair + 1)
                d.wait_ge(L["pack"], UNITS * GB * g + UNITS * (2 * pair + 2) + UNITS)
                d.tensor_copy(ddum[:, :], eps_t[:, :])
                for b in bs:
                    d.max(t16[:, k, b, 0:8], bank[b % 2][:, 0:KEY])
                d.drain()
                for b in bs:
                    d.match_replace(key[:, b % 2, :], t16[:, k, b, 0:8], bank[b % 2][:, 0:KEY], -1.0) \
                        .then_inc(L["key"], 1)
                d.drain()
                for b in bs:
                    d.max(t16[:, k, b, 8:16], key[:, b % 2, :])
                d.drain()

            def edge_list(g, k, at_):
                ti, tw = ia.bitcast(I32), ib.bitcast(I32)
                if at_:
                    d.wait_ge(L["es"], at_[0] + 1)
                    d.scalar_tensor_tensor(es, pr, -1e30, es_sums, ALU.mult, ALU.add)
                then(d, d.tensor_copy(ti, t16[:, k, :, :]))
                if at_:
                    d.tensor_reduce(sm[:, 0, :], es, AX, ALU.max)
                then(d, d.tensor_scalar(ti, ti, KEY - 1, None, ALU.bitwise_and))
                if at_:
                    d.tensor_scalar(sm[:, 1, :], sm[:, 0, :], -1.0, None, ALU.mult)
                    d.tensor_copy(m3[:, :, 0], sm[:, 0, :])
                d.tensor_copy(cf, ti)
                if at_:
                    d.drain().then_inc(L["smax"], 1)
                    d.tensor_tensor(sm[:, 4, :], sm[:, 0, :], m3[:, :, 0], ALU.subtract)
                else:
                    d.drain()
                then(d, d.tensor_tensor(wf, t16[:, k, :, :], cf, ALU.subtract))
                if at_:
                    d.tensor_copy(m3[:, :, 1], sm[:, 4, :])
                then(d, d.tensor_scalar(tp.bitcast(I32), wf.bitcast(I32), MASK, None, ALU.bitwise_and))
                if at_:
                    d.tensor_tensor(m3[:, :, 2], sm[:, 4, :], m3[:, :, 1], ALU.subtract)
                    d.drain().then_inc(L["m3"], 1)
                for v in range(BPW):
                    if v + 1 < BPW:
                        d.tensor_tensor(r1, (wf, r1)[v > 0], tp, ALU.subtract)
                    then(d, d.tensor_tensor(e48[:, :, v * SLOTS:(v + 1) * SLOTS], tp, cf, ALU.add))
                    if v + 1 < BPW:
                        then(d, d.tensor_scalar(tp.bitcast(I32), r1.bitcast(I32), MASK, None, ALU.bitwise_and))
                for b in range(GB):
                    d.max(s16[:, b, 0:8], e48[:, b, :])
                d.drain()
                for b in range(GB):
                    d.match_replace(e48[:, b, :], s16[:, b, 0:8], e48[:, b, :], -1.0)
                d.drain()
                for b in range(GB):
                    d.max(s16[:, b, 8:16], e48[:, b, :])
                d.drain()
                d.tensor_scalar(wf, s16, float(KEY), None, ALU.is_ge)
                d.tensor_scalar(tw, s16.bitcast(I32), 23, None, ALU.logical_shift_right)
                d.tensor_reduce(alpha[:, grp(g)], cnt[:, k, :, :], AX, ALU.add)
                then(d, d.tensor_copy(ti, s16))
                d.tensor_reduce(nv[:, k, :], wf, AX, ALU.add)
                then(d, d.tensor_scalar(ti, ti, KEY - 1, None, ALU.bitwise_and))
                d.tensor_copy(nvb, nv[:, k, :])
                d.drain().then_inc(L["nv"], 1)
                d.tensor_tensor(sm[:, 5, :], alpha[:, grp(g)], nv[:, k, :], ALU.not_equal)
                d.tensor_scalar(vt[:, :, 0:SLOTS], tw, EXP, None, ALU.subtract)
                d.tensor_copy(vt[:, :, SLOTS:2 * SLOTS], ti)
                d.drain()

            def edges(g, k):
                d.wait_ge(L["start"], g + 1)
                then(d, d.tensor_copy(ends[:, 0, :], bank[2][:, 0:GB]))
                d.tensor_copy(vt[:, :, 2 * SLOTS:2 * SLOTS + 1].rearrange("p b o -> p (b o)"), ends[:, 0, :])
                d.tensor_copy(first_e[:, grp(g)], ends[:, 0, :])
                then(d, d.tensor_tensor(ends[:, 1, :], ends[:, 0, :], nv[:, k, :], ALU.add))
                d.tensor_copy(last_e[:, grp(g)], ends[:, 1, :])
                d.scalar_tensor_tensor(bad[:, grp(g)], ends[:, 1, :], float(EW), sm[:, 5, :], ALU.is_gt, ALU.max)
                for b in range(GB):
                    d.tensor_scalar(am1[:, b, :], iow, ends[:, 1, b:b + 1], None, ALU.is_lt)
                d.drain()
                for b in range(GB):
                    d.scalar_tensor_tensor(am[:, k, b, :], iow, ends[:, 0, b:b + 1], am1[:, b, :],
                                           ALU.is_ge, ALU.mult).then_inc(L["m"], 1)
                for v in range(2):
                    half = slice(v * GT // 2, (v + 1) * GT // 2)
                    sel = bank[2 + v][:, 0:33 * GT // 2].rearrange("p (n s) -> p n s", s=33)
                    d.wait_ge(L["v"], 2 * g + v + 1)
                    d.tensor_tensor(rr[:, half].rearrange("p (b q) -> p b q", q=TILES), bc(posc, [P, 2, TILES], 1),
                                    sel[:, :, 32].rearrange("p (b q) -> p b q", q=TILES), ALU.subtract)
                    d.tensor_copy(jt[:, half, :], sel[:, :, SLOTS:2 * SLOTS])
                d.drain()
                for v in range(2):
                    half = slice(v * GT // 2, (v + 1) * GT // 2)
                    sel = bank[2 + v][:, 0:33 * GT // 2].rearrange("p (n s) -> p n s", s=33)
                    d.scalar_tensor_tensor(jt[:, half, :], sel[:, :, 0:SLOTS], float(KEY), jt[:, half, :], ALU.mult,
                                           ALU.add)
                then(d, d.tensor_tensor(oh[:, k, :, :], bc(iok[:, 0:SLOTS], [P, GT, SLOTS], 1),
                                        bc(rr, [P, GT, SLOTS], 2), ALU.is_equal))
                then(d, d.tensor_tensor(jt, jt, oh[:, k, :, :], ALU.mult))
                then(d, d.tensor_reduce(jj, jt, AX, ALU.add))
                d.tensor_scalar(ix[:, k, :], jj, 0.0, float(N - 1), ALU.max, ALU.min)
                d.drain().then_inc(L["idx"], 1)
                d.tensor_copy(idx[:, bass.ds(g * GT, GT) if not isinstance(g, int) else slice(g * GT, g * GT + GT)],
                              ix[:, k, :])

            def dots(g, k, first, last):
                for p in range(first, last):
                    for n in (2 * p, 2 * p + 1):
                        if n % TILES == 0:
                            d.wait_ge(L["gat"][k][n // TILES], 8 * TILES * (g - k) + 16 * TILES)
                        if n % 2 == 0 and p >= 2:
                            d.wait_ge(L["dot"], GT * g + n - 2)
                        d.wait_ge(L["exp_g"], GT // 2 * g + p + 1)
                        d.tensor_tensor_reduce(out=junk[:, n % 4, :], in0=gat[:, k, n, :],
                                               in1=bank[EB[p % 3]][:, n % 2 * D:(n % 2 + 1) * D],
                                               scale=1.0, scalar=0.0, op0=ALU.mult, op1=ALU.add,
                                               accum_out=ee[:, 0, n:n + 1]).then_inc(L["dot"], 1)

            def by_slot(g, k):
                d.drain()
                e, r = ee[:, 0, :], ee[:, 1, :]
                then(d, d.tensor_copy(e3[:, :, 0], e))
                d.tensor_tensor(pr, bc(iok[:, 0:SLOTS], [P, GB, SLOTS], 1),
                                bc(nv[:, k, :], [P, GB, SLOTS], 2), ALU.is_ge)
                then(d, d.tensor_tensor(r, e, e3[:, :, 0], ALU.subtract))
                then(d, d.tensor_copy(e3[:, :, 1], r))
                then(d, d.tensor_tensor(e3[:, :, 2], r, e3[:, :, 1], ALU.subtract))
                d.tensor_tensor(oe, bc(oh[:, k, :, :], [P, GT, 3, SLOTS], 2),
                                bc(e3[:, :, 0:3], [P, GT, 3, SLOTS], 3), ALU.mult)
                d.drain().then_inc(L["ohe"], 1)

            es_sums = bank[2][:, 0:GB * SLOTS].rearrange("p (b s) -> p b s", s=SLOTS)

            def row_max(g, k):
                d.wait_ge(L["es"], g + 1)
                then(d, d.scalar_tensor_tensor(es, pr, -1e30, es_sums, ALU.mult, ALU.add))
                then(d, d.tensor_reduce(sm[:, 0, :], es, AX, ALU.max))
                d.tensor_scalar(sm[:, 1, :], sm[:, 0, :], -1.0, None, ALU.mult)
                then(d, d.tensor_copy(m3[:, :, 0], sm[:, 0, :]))
                d.drain().then_inc(L["smax"], 1)
                then(d, d.tensor_tensor(sm[:, 4, :], sm[:, 0, :], m3[:, :, 0], ALU.subtract))
                then(d, d.tensor_copy(m3[:, :, 1], sm[:, 4, :]))
                d.tensor_tensor(m3[:, :, 2], sm[:, 4, :], m3[:, :, 1], ALU.subtract)
                d.drain().then_inc(L["m3"], 1)

            def weights(g, k):
                d.wait_ge(L["den"], g + 1)
                d.reciprocal(sm[:, 4, :], sm[:, 2, :])
                d.wait_ge(L["mx"], g + 1)
                then(d, d.tensor_reduce(ee[:, 1, :], bank[3][:, 0:4 * GT].rearrange("p (n s) -> p n s", s=4)[:, :, 0:3],
                                        AX, ALU.add))
                d.tensor_tensor(ee[:, 1, :], ee[:, 0, :], ee[:, 1, :], ALU.subtract)
                d.tensor_tensor(sm[:, 3, :], sm[:, 4, :], natt[:, grp(g)], ALU.mult)
                d.drain().then_inc(L["less"], 1)
                d.wait_ge(L["agg"], GB * g + 2 * GB)
                d.wait_ge(L["pexp"], g + 1)
                d.tensor_tensor(otp[:, 0:BY_DVE, :], ot[:, 0:BY_DVE, :],
                                bc(pe_[:, 0:BY_DVE], [P, BY_DVE, P], 2), ALU.mult)
                d.drain().then_inc(L["otp"], 1)

            def new_x(g, k, b):
                d.wait_ge(L["xb"], g + 1)
                d.wait_ge(L["proj"], GB * g + b // 2 * 2 + 4)
                d.scalar_tensor_tensor(x1[:, at(g * GB + b), :],
                                       bank[7 - b // 2][:, b % 2 * D:(b % 2 + 1) * D], sm[:, 3, b:b + 1],
                                       xr2[:, k, b, :], ALU.mult, ALU.add).then_inc(L["x1"], 1)

            def body(wd, ls, at_, ag_):
                if ls and not at_:
                    d.wait_ge(s_all, 1)
                    d.tensor_scalar(cs(1)[:, 1:2], cs(1)[:, 0:1], -1.0, None, ALU.mult)
                    d.drain().then_inc(s_negmax, 1)
                if ls and not at_:
                    for k in (0, 1):
                        d.wait_ge(s_th[k], 16 * NG // 2)
                if ls:
                    edges(*ls)
                if at_ and not ag_:
                    d.wait_ge(s_all, 2)
                    d.reciprocal(cs(1)[:, 3:4], cs(1)[:, 2:3])
                    d.drain()
                    d.tensor_scalar(natt[:, :], natt[:, :], cs(1)[:, 3:4], None, ALU.mult)
                if ag_:
                    new_x(*ag_, 0)
                    new_x(*ag_, 1)
                if at_:
                    dots(*at_, 0, GT // 4)
                if wd:
                    keys(*wd, 0)
                if at_:
                    dots(*at_, GT // 4, GT // 2)
                    by_slot(*at_)
                if wd:
                    keys(*wd, 1)
                if wd:
                    edge_list(*wd, at_)
                elif at_:
                    row_max(*at_)
                if ag_:
                    new_x(*ag_, 2)
                    new_x(*ag_, 3)
                if at_:
                    weights(*at_)
            staged(d, body)
            d.drain()
            then(d, d.tensor_reduce(badc[:, 0:1], bad[:, :], AX, ALU.max))
            d.drain().then_inc(L["flag1"], 1)

        mx, o = arena(0, NB, D)
        ys, o = arena(o, NB, DYP)
        ys = ys.rearrange("p (g b) d -> p g b d", g=NG)
        sq, o = arena(o, GB, D)
        assert o <= WORK, o
        s_sq = sem("s_sq")
        s_sq1 = sem("s_sq1")
        s_gm = sem("s_gm")
        s_ysz = sem("s_ysz")
        s_ys = [sem("s_ys_act"), sem("s_ys_dve")]
        s_tyo = sem("s_tyo")
        s_asked = sem("s_asked")
        s_answered = sem("s_answered")
        asked, answered = [0], [0]

        def ask(d):
            asked[0] += 1
            d.drain().then_inc(s_asked, 1)
            d.wait_ge(s_answered, asked[0])

        def answer(a, o_, i_, func, then_func=None):
            answered[0] += 1
            a.wait_ge(s_asked, answered[0])
            a.activation(o_, i_, func)
            a.drain().then_inc(s_answered, 1)
            if then_func is not None:
                a.activation(tab[:, :], eps_t[:, :], then_func)

        def then(d, ins):
            d.drain()

        def root(d, i_):
            d.tensor_scalar(i_, i_, EPS * EPS, None, ALU.max)
            ask(d)

        def artanh(d, o_, i_, y, u, t):
            then(d, d.tensor_scalar(y, i_, CLIP, None, ALU.min))
            then(d, d.tensor_scalar(u, y, -1.0, 1.0, ALU.mult, ALU.add))
            then(d, d.reciprocal(t, u))
            then(d, d.scalar_tensor_tensor(y, y, 2.0, t, ALU.mult, ALU.mult))
            d.tensor_scalar(u, y, 1.0, None, ALU.add)
            ask(d)
            then(d, d.tensor_scalar(u, u, 1.0, None, ALU.subtract))
            then(d, d.tensor_scalar(t, u, 0.0, None, ALU.is_equal))
            d.tensor_tensor(u, u, t, ALU.add)
            then(d, d.tensor_tensor(o_, o_, t, ALU.add))
            then(d, d.reciprocal(t, u))
            then(d, d.scalar_tensor_tensor(o_, o_, 0.5, t, ALU.mult, ALU.mult))
            then(d, d.tensor_tensor(o_, o_, y, ALU.mult))

        S1, S2, XN, MN, ATH, Z, TH, R, Q, GAM, GR, GM1, T1, T2, T3 = (cs(k) for k in range(15))

        def mobius_dve(d):
            root(d, S1)
            root(d, S2)
            artanh(d, ATH, XN, T1, T2, T3)
            then(d, d.reciprocal(T1, XN))
            then(d, d.tensor_tensor(T1, T1, MN, ALU.mult))
            d.tensor_tensor(Z, T1, ATH, ALU.mult)
            ask(d)
            then(d, d.reciprocal(T1, MN))
            d.tensor_tensor(R, TH, T1, ALU.mult)
            then(d, d.tensor_scalar(T2, MN, EPS, None, ALU.is_gt))
            then(d, d.tensor_tensor(R, R, T2, ALU.mult))
            then(d, d.tensor_tensor(Q, R, R, ALU.mult))
            then(d, d.tensor_tensor(Q, Q, S2, ALU.mult))
            then(d, d.tensor_scalar(Q, Q, -1.0, 1.0, ALU.mult, ALU.add))
            then(d, d.reciprocal(T1, Q))
            then(d, d.tensor_scalar(GAM, T1, 2.0, 1e-15, ALU.mult, ALU.max))
            d.tensor_tensor(GR, GAM, R, ALU.mult)
            then(d, d.tensor_scalar(GM1, GAM, 1.0, None, ALU.subtract))

        def mobius_act(a):
            answer(a, XN, S1, ACT.Sqrt)
            answer(a, MN, S2, ACT.Sqrt, ACT.Ln)
            answer(a, ATH, T2, ACT.Ln, ACT.Tanh)
            answer(a, TH, Z, ACT.Tanh)

        nom, nom_end = arena(0, NB, DY)
        yr, o = arena(nom_end, NB, DYP)
        ad2, o = arena(o, N)
        at2, o = arena(o, 2, CH)
        assert o <= WORK, o
        M = {n: sem("gm_" + n) for n in ("y", "adj", "adj_used", "t", "tc", "nom", "nomc", "alpha")}

        def gm_sp(e):
            e.dma_start(yr, ty_r).then_inc(M["y"], 16)
            with e.Fori(0, NB) as i:
                e.wait_ge(M["t"], NCH * (i + 1))
                e.wait_ge(M["alpha"], i + 1)
                e.dma_start(ad2, adj[bass.ds(i * P, P), :]).then_inc(M["adj"], 16)

        def gm_pe(t):
            t.sem_inc(M["t"], NCH)
            t.wait_ge(M["y"], 16)
            with t.Fori(0, NB) as i:
                t.wait_ge(M["adj"], 16 * (i + 1))
                t.wait_ge(M["nomc"], i + 1)

                def add_chunk(c):
                    t.wait_ge(M["tc"], NCH * i + c + 1)
                    for q in range(TPC):
                        n = c * TPC + q
                        last = t.matmul(bank[5][:, 0:DY], at2[:, c % 2, q * P:(q + 1) * P], yr[:, n, 0:DY],
                                        start=(n == 0), stop=(n == NB - 1))
                    return last

                for c in range(NCH):
                    for q in range(TPC):
                        n = c * TPC + q
                        last = t.transpose(bank[3 + c % 2][:, q * P:(q + 1) * P], ad2[:, n * P:(n + 1) * P],
                                           ident[:, :])
                    last.then_inc(M["t"], 1)
                    if c:
                        add_chunk(c - 1)
                add_chunk(NCH - 1).then_inc(M["nom"], 1)

        def gm_act(a):
            a.sem_inc(M["nomc"], 1)
            with a.Fori(0, NB) as i:
                for c in range(NCH):
                    a.wait_ge(M["t"], NCH * (i + 1) + c + 1)
                    a.activation(at2[:, c % 2, :], bank[3 + c % 2][:, :], ACT.Copy).then_inc(M["tc"], 1)
                a.wait_ge(M["nom"], i + 1)
                a.activation(nom[:, bass.ds(i, 1), :], bank[5][:, 0:DY], ACT.Copy)
                a.drain().then_inc(M["nomc"], 1)

        def gm_dve(d):
            d.sem_inc(M["alpha"], 1)
            with d.Fori(0, NB) as i:
                d.wait_ge(M["adj"], 16 * (i + 1))
                d.tensor_reduce(alpha[:, bass.ds(i, 1)], ad2, AX, ALU.add).then_inc(M["alpha"], 1)
            d.wait_ge(M["nomc"], NB + 1)
            with d.Fori(0, NB) as i:
                squares(d, i)
                d.drain()

        def squares(d, n):
            v = nom[:, at(n), 0:D]
            d.scalar_tensor_tensor(fs[:, 0, :], v, 0.0, v, ALU.max, ALU.mult, accum_out=SP[:, at(n)])
            d.scalar_tensor_tensor(fs[:, 1, :], v, 0.0, v, ALU.min, ALU.mult, accum_out=SN[:, at(n)])

        assert nom_end <= WORK
        gt2, o = arena(nom_end, 2 * GT, DYP)
        gt2 = gt2.rearrange("p (k n) d -> p k n d", k=2)
        otf, o = arena(o, 2 * TILES, P)
        otf = otf.rearrange("p (k q) n -> p k q n", k=2)
        iow2, o = arena(o, EW, dt=F16)
        idb2, o = arena(o, P, dt=BF16)
        mm2, o = arena(o, 2, EW, dt=BF16)
        mm1, o = arena(o, EW, dt=BF16)
        ix2f, o = arena(o, 2, GT)
        se2, o = arena(o, 2, 2 * GB)
        assert o <= WORK, o
        ix2 = ix2f.bitcast(I32)
        F = {n: sem("fm_" + n) for n in (
            "const",
            "idx",
            "m",
            "t",
            "tc",
            "nom",
            "nomc")}
        F["gat"] = [[sem(f"fm_gat{k}{b}") for b in range(GB)] for k in range(2)]

        def fm_pool(p):
            p.iota(iow2, pattern=[[1, EW]], base=0, channel_multiplier=0, allow_small_or_imprecise_dtypes=True)
            p.tensor_copy(idb2, ident[:, :])
            p.drain().then_inc(F["const"], 1)
            with p.Fori(0, NG // 2) as j:
                for k in (0, 1):
                    g = 2 * j + k
                    p.wait_ge(F["idx"], g + 1)
                    p.wait_ge(F["nom"], GB * g + GB)
                    p.sem_inc(s_go, 1)
                    for n in range(GT):
                        p.indirect_dma_start(gt2[:, k, n, :], None, table_y,
                                             bass.IndirectOffsetOnAxis(ix2[:, k, n:n + 1], 0)) \
                            .then_inc(F["gat"][k][n // TILES], 16)

        def fm_dve(d):
            d.sem_inc(F["m"], 2)
            d.wait_ge(F["const"], 1)

            def group(g, k, squared):
                d.wait_ge(F["nom"], GB * g + GB)
                d.tensor_copy(ix2[:, k, :], idx[:, bass.ds(g * GT, GT) if not isinstance(g, int)
                                                else slice(g * GT, (g + 1) * GT)])
                d.tensor_copy(se2[:, k, 0:GB], first_e[:, grp(g)])
                d.tensor_copy(se2[:, k, GB:2 * GB], last_e[:, grp(g)])
                d.drain().then_inc(F["idx"], 1)
                for b in range(GB):
                    d.wait_ge(F["t"], GB * g + b + 1)
                    then(d, d.tensor_scalar(mm1, iow2, se2[:, k, GB + b:GB + b + 1], None, ALU.is_lt))
                    d.scalar_tensor_tensor(mm2[:, b % 2, :], iow2, se2[:, k, b:b + 1], mm1, ALU.is_ge, ALU.mult)
                    d.drain().then_inc(F["m"], 1)
                    if squared:
                        d.wait_ge(F["nomc"], GB * g - GB + b + 3)
                        squares(d, g * GB - GB + b)

            group(0, 0, False)
            group(1, 1, True)
            with d.Fori(0, NG // 2 - 1) as j:
                for k in (0, 1):
                    group(2 * j + 2 + k, k, True)
            for b in range(GB):
                n = NB - GB + b
                d.drain()
                d.wait_ge(F["nomc"], n + 3)
                squares(d, n)

        def fm_pe(t):
            t.sem_inc(F["t"], 2)
            t.sem_inc(F["nom"], 2 * GB)
            t.wait_ge(F["const"], 1)
            with t.Fori(0, NG // 2) as j:
                for k in (0, 1):
                    g = 2 * j + k
                    for b in range(GB):
                        t.wait_ge(F["m"], GB * g + b + 3)
                        t.wait_ge(F["tc"], GB * g + b + 1)
                        tb = bank[6 + b % 2][:, :].bitcast(BF16)
                        for q in range(TILES):
                            last = t.transpose(tb[:, q * P:(q + 1) * P], mm2[:, b % 2, q * P:(q + 1) * P], idb2)
                        last.then_inc(F["t"], 1)
                        t.wait_ge(F["tc"], GB * g + b + 3)
                        t.wait_ge(F["gat"][k][b], 8 * TILES * (g - k) + 16 * TILES)
                        t.wait_ge(F["nomc"], GB * g + b + 1)
                        for q in range(TILES):
                            last = t.matmul(bank[4 + b % 2][:, 0:DY], otf[:, b % 2, q, :],
                                            gt2[:, k, b * TILES + q, 0:DY], start=(q == 0), stop=(q == TILES - 1))
                        last.then_inc(F["nom"], 1)

        def fm_act(a):
            a.sem_inc(F["tc"], 2)
            a.sem_inc(F["nomc"], 2)
            with a.Fori(0, NG // 2) as j:
                for k in (0, 1):
                    g = 2 * j + k
                    for b in range(GB):
                        a.wait_ge(F["t"], GB * g + b + 3)
                        a.wait_ge(F["nom"], GB * g + 2 * GB + b - 1)
                        a.activation(otf[:, b % 2, :, :],
                                     bank[6 + b % 2][:, :].bitcast(BF16)[:, 0:EW].rearrange("p (q n) -> p q n", q=TILES),
                                     ACT.Copy).then_inc(F["tc"], 1)
                        a.wait_ge(F["nom"], GB * g + 2 * GB + b + 1)
                        a.activation(nom[:, at(g * GB + b), :], bank[4 + b % 2][:, 0:DY], ACT.Copy)
                        a.drain().then_inc(F["nomc"], 1)

        S0, DN, RD, S4, WW, NN, TA, SS1, FF, S5, F3, U1, U2, U3, U4, SP, SN = (cs(k) for k in range(17))
        den = nom[:, :, D]

        def midpoint_dve(d):
            d.tensor_tensor(S0, SP, SN, ALU.add)
            then(d, d.tensor_scalar(U1, den, 0.0, None, ALU.is_ge))
            then(d, d.tensor_scalar(U1, U1, 2.0, -1.0, ALU.mult, ALU.add))
            then(d, d.tensor_tensor(DN, den, U1, ALU.mult))
            then(d, d.scalar_tensor_tensor(DN, DN, EPS, U1, ALU.max, ALU.mult))
            then(d, d.reciprocal(RD, DN))
            then(d, d.tensor_tensor(S4, S0, RD, ALU.mult))
            then(d, d.tensor_tensor(S4, S4, RD, ALU.mult))
            then(d, d.tensor_scalar(U1, S4, -1.0, 1.0, ALU.mult, ALU.add))
            d.tensor_scalar(U1, U1, EPS, None, ALU.max)
            ask(d)
            then(d, d.tensor_scalar(U2, U2, 1.0, None, ALU.add))
            then(d, d.reciprocal(WW, U2))
            then(d, d.tensor_tensor(U4, WW, WW, ALU.mult))
            then(d, d.tensor_tensor(U4, U4, S4, ALU.mult))
            then(d, d.tensor_copy(U1, U4))
            root(d, U1)
            artanh(d, TA, NN, U1, U2, U3)
            d.tensor_tensor(TA, TA, alpha[:, :], ALU.mult)
            ask(d)
            then(d, d.reciprocal(U1, NN))
            then(d, d.tensor_tensor(SS1, TA, U1, ALU.mult))
            then(d, d.tensor_tensor(U4, U4, SS1, ALU.mult))
            then(d, d.tensor_tensor(U4, U4, SS1, ALU.mult))
            root(d, U4)
            artanh(d, TA, NN, U1, U2, U3)
            then(d, d.reciprocal(U1, NN))
            then(d, d.tensor_tensor(FF, TA, U1, ALU.mult))
            then(d, d.tensor_tensor(FF, FF, SS1, ALU.mult))
            then(d, d.tensor_tensor(FF, FF, WW, ALU.mult))
            then(d, d.tensor_tensor(FF, FF, RD, ALU.mult))
            then(d, d.tensor_scalar(U1, FF, 0.0, None, ALU.is_ge))
            d.tensor_scalar(U2, U1, -1.0, 1.0, ALU.mult, ALU.add)
            then(d, d.tensor_tensor(S5, SP, U1, ALU.mult))
            then(d, d.tensor_tensor(U2, SN, U2, ALU.mult))
            then(d, d.tensor_tensor(S5, S5, U2, ALU.add))
            then(d, d.tensor_tensor(S5, S5, FF, ALU.mult))
            then(d, d.tensor_tensor(S5, S5, FF, ALU.mult))
            root(d, S5)
            ask(d)
            then(d, d.reciprocal(U1, NN))
            then(d, d.tensor_tensor(F3, TA, U1, ALU.mult))
            then(d, d.tensor_tensor(F3, F3, FF, ALU.mult))

        def midpoint_act(a):
            a.activation(tab[:, :], eps_t[:, :], ACT.Sqrt)
            a.drain()
            answer(a, U2, U1, ACT.Sqrt)
            answer(a, NN, U1, ACT.Sqrt, ACT.Ln)
            answer(a, TA, U2, ACT.Ln, ACT.Tanh)
            answer(a, TA, TA, ACT.Tanh, ACT.Sqrt)
            answer(a, NN, U4, ACT.Sqrt, ACT.Ln)
            answer(a, TA, U2, ACT.Ln, ACT.Sqrt)
            answer(a, NN, S5, ACT.Sqrt, ACT.Tanh)
            answer(a, TA, NN, ACT.Tanh)

        s_u = sem("s_u")
        s_us = sem("s_us")
        s_o = sem("s_o")
        s_out = sem("s_out")

        block = ctx.enter_context(nc.Block())

        @block.sync
        def _(e):
            def load(g, k):
                e.wait_ge(f0.x_used, g + 1)
                e.dma_start(xs[:, k, :, :], x_r[:, grp(g), :]).then_inc(f0.x_in[k], 16)

            load(0, 0)
            e.dma_start(ew, edge_w.rearrange("(c p) d -> p c d", p=P)).then_inc(s_w, 16)
            e.dma_start(nw, node_w.rearrange("(c p) d -> p (c d)", p=P), allow_slow_non_contiguous=True).then_inc(s_w, 16)
            load(1, 1)
            e.dma_start(w0[:, :, :], weight.rearrange("(c p) d -> p c d", p=P)).then_inc(s_w2, 16)
            e.dma_start(w1[:, :, :], W1.rearrange("(c p) d -> p c d", p=P)).then_inc(s_w2, 16)
            e.dma_start(bias_bc[:, :], bias.rearrange("(a d) -> a d", a=1).broadcast_to([P, D])).then_inc(s_w2, 16)
            for n in range(2):
                for h in range(UNITS):
                    e.dma_start(adu[:, n, h, :], adj[n * P:(n + 1) * P, h * UW:(h + 1) * UW]).then_inc(L["adj"][n][h], 16)

            def store(g, k):
                e.wait_ge(f0.h, GB * (g + 1))
                e.dma_start(th_r[:, grp(g), :], hs[:, k, :, :]).then_inc(s_th[k], 16)
            with e.Fori(0, (NG - 2) // 2) as j:
                for k in (0, 1):
                    store(2 * j + k, k)
                    load(2 * j + k + 2, k)
            store(NG - 2, 0)
            store(NG - 1, 1)
            fast_load(e)
            barrier(e)
            general_if(e, ga_sp)
            barrier(e)

            for g in range(NG):
                e.wait_ge(s_ys[g % 2], g // 2 + 1)
                e.dma_start(ty_r[:, grp(g), :], ys[:, g, :, :]).then_inc(s_tyo, 16)
            e.wait_ge(s_tyo, 16 * NG)
            barrier(e)
            general_if(e, gm_sp)
            barrier(e)
            for g in range(NG):
                e.wait_ge(s_o, GB * (g + 1))
                e.dma_start(out_r[:, grp(g), :], x1[:, grp(g), :]).then_inc(s_out, 16)
            e.wait_ge(s_out, 16 * NG)

        @block.gpsimd
        def _(p):
            p.memset(ident[:, :], 0.0)
            p.memset(eps_t[:, :], LN_EPS)
            p.drain()
            p.affine_select(out=ident[:, :], in_=ident[:, :], compare_op=ALU.not_equal, fill=1.0, base=0,
                            pattern=[[-1, P]], channel_multiplier=1)
            p.drain().then_inc(s_ident, 1)
            fast_constants(p)

            def split(g, k):
                for b in (2, 3):
                    p.wait_ge(s_rest, GB * g + b + 1)
                    p.tensor_copy(gx_b[:, at(g * GB + b), D:2 * D], res[:, k, b, :])
                p.drain()
                for b in (2, 3, 0, 1):
                    if b == 0:
                        p.wait_ge(s_mid, g + 1)
                    blk = at(g * GB + b)
                    p.tensor_tensor(gx_b[:, blk, 2 * D:3 * D], res[:, k, b, :], gx_b[:, blk, D:2 * D],
                                    ALU.subtract)
                p.drain().then_inc(s_restfree, 1)
            p.sem_inc(s_restfree, 2)
            with p.Fori(0, NG // 2) as j:
                split(2 * j, 0)
                split(2 * j + 1, 1)
            p.wait_ge(s_red, 1)
            p.partition_all_reduce(cs(1)[:, 0:1], cs(0)[:, 0:1], P, RMAX)
            p.drain().then_inc(s_all, 1)
            p.wait_ge(s_exp, 1)
            p.partition_all_reduce(cs(1)[:, 2:3], cs(0)[:, 2:3], P, RADD)
            p.drain().then_inc(s_all, 1)
            p.wait_ge(s_w2, 48)
            for k in (0, 1):
                p.wait_ge(s_th[k], 16 * NG // 2)
            p.wait_ge(f0.x_used, NG + 2)
            fast_pool(p)
            fast_flag(p)
            barrier(p)
            general_if(p)
            barrier(p)
            p.memset(ys[:, :, :, D:DYP], 0.0)
            p.drain().then_inc(s_ysz, 1)
            barrier(p)
            general_if(p, None, fm_pool)
            barrier(p)

        @block.scalar
        def _(a):
            a.sem_inc(f0.x_used, 2)
            a.wait_ge(s_ident, 1)

            def first(st, nm, tr, pd):
                def hi(b):
                    if pd:
                        g, k = pd
                        a.wait_ge(f0.prod, GB * (g + 2) + b + 1)
                        a.activation(gx_b[:, at(g * GB + b), 0:D], bank[2 + b][:, 0:D], ACT.Copy).then_inc(s_hi, 1)
                hi(0)
                if nm:
                    g, k = nm
                    if not isinstance(g, int) or g >= 2:
                        a.wait_ge(s_th[k], 8 * (g - k))
                    front_norm(a, f0, xs[:, k, :, :], g, k)
                    a.drain().then_inc(f0.x_used, 1)
                hi(1)
                if st:
                    front_std(a, f0, st[0])
                hi(2)
                hi(3)
                if pd:
                    g, k = pd
                    for b in (0, 1):
                        a.wait_ge(s_rest, GB * g + b + 1)
                        a.activation(gx_b[:, at(g * GB + b), D:2 * D], res[:, k, b, :], ACT.Copy)
                    a.drain().then_inc(s_mid, 1)
            staged(a, first)
            fast_act(a)
            barrier(a)
            general_if(a, ga_act)
            barrier(a)

            def second(st, nm, tr, pd):
                def mx_out(b):
                    if pd:
                        g, k = pd
                        a.wait_ge(f1.prod, GB * (g + 2) + b + 1)
                        a.activation(mx[:, at(g * GB + b), :], bank[2 + b][:, 0:D], ACT.Copy)
                        a.activation(fs[:, b % 2, :], bank[2 + b][:, 0:D], ACT.Square,
                                     accum_out=S2[:, at(g * GB + b)])
                        if b % 2:
                            a.drain()
                mx_out(0)
                if nm:
                    g, k = nm
                    if not isinstance(g, int) or g >= 2:
                        a.wait_ge(s_sq1, g - 1)
                    front_norm(a, f1, x1[:, grp(g), :], g, k)
                mx_out(1)
                if st:
                    front_std(a, f1, st[0])
                mx_out(2)
                mx_out(3)
                if pd:
                    a.sem_inc(f1.prod_used, 1)
            a.sem_inc(f1.prod_used, 1)
            staged(a, second)
            a.drain().then_inc(s_sq, 1)
            mobius_act(a)
            a.wait_ge(s_gm, 1)
            a.wait_ge(s_ysz, 1)
            for g in range(0, NG, 2):
                for b in range(GB):
                    n = g * GB + b
                    a.activation(ys[:, g, b, 0:D], mx[:, n, :], ACT.Copy, scale=GR[:, n:n + 1])
                a.activation(ys[:, g, :, D], GM1[:, g * GB:g * GB + GB], ACT.Copy)
                a.drain().then_inc(s_ys[0], 1)
            barrier(a)
            general_if(a, gm_act, fm_act)
            barrier(a)
            midpoint_act(a)
            a.wait_ge(s_u, 1)
            for n in range(NB):
                a.activation(nom[:, n, 0:D], nom[:, n, 0:D], ACT.Relu, scale=F3[:, n:n + 1]).then_inc(s_us, 1)

        @block.tensor
        def _(t):
            for f in (f0, f1):
                t.sem_inc(f.t, 2 * GB)
                t.sem_inc(f.prod, 2 * GB)
            t.wait_ge(s_ident, 1)
            t.wait_ge(s_w, 32)
            for r in range(KD):
                for c in range(KD):
                    last = t.transpose(bank[6][:, (c * KD + r) * P:(c * KD + r + 1) * P],
                                       ew[:, r, c * P:(c + 1) * P], ident[:, :])
            last.then_inc(s_ewT, 1)
            t.wait_ge(s_ewTc, 1)
            for r in range(KD):
                for c in range(KD):
                    last = t.matmul(bank[7][:, r * D:(r + 1) * D], ewT[:, c, r * P:(r + 1) * P], ewT[:, c, :],
                                    start=(c == 0), stop=(c == KD - 1))
            last.then_inc(s_eet, 1)
            t.wait_ge(s_eet, 2)

            def front_pe(f, rhs, n):
                def steps(st, nm, tr, pd):
                    if tr:
                        front_transpose(t, f, *tr)
                    if pd:
                        front_product(t, f, rhs, n, *pd)
                return steps
            staged(t, front_pe(f0, rhs_g, DY))
            t.wait_ge(s_hi, NB)
            t.wait_ge(f0.prod_used, NG + 1)
            t.wait_ge(s_w2, 48)
            fast_pe(t)
            barrier(t)
            general_if(t, ga_pe)
            barrier(t)
            staged(t, front_pe(f1, w1, D))
            barrier(t)
            general_if(t, gm_pe, fm_pe)
            barrier(t)

        @block.vector
        def _(d):
            for f in (f0, f1):
                d.sem_inc(f.hT, 1)
            d.sem_inc(f0.prod_used, 1)

            def first(st, nm, tr, pd):
                def rest(b):
                    if pd:
                        g, k = pd
                        if b == 0:
                            d.wait_ge(s_restfree, g + 1)
                        d.wait_ge(s_hi, GB * g + b + 1)
                        d.tensor_tensor(res[:, k, b, :], bank[2 + b][:, 0:D], gx_b[:, at(g * GB + b), 0:D],
                                        ALU.subtract).then_inc(s_rest, 1)
                        d.tensor_copy(logit[:, at(g * GB + b)], bank[2 + b][:, D:DY])

                if tr:
                    front_hT(d, f0, *tr)
                if nm:
                    front_scale(d, f0, nm[0])
                rest(0)
                if st:
                    g, k = st
                    d.wait_ge(f0.x_in[k], 8 * (g - k) + 16)
                    front_stats(d, f0, xs[:, k, :, :], g)
                rest(1)
                rest(2)
                rest(3)
                if pd:
                    d.drain().then_inc(f0.prod_used, 1)
                if nm and not tr:
                    d.wait_ge(s_ewT, 1)
                    d.tensor_copy(ewT.rearrange("p a b -> p (a b)"), bank[6][:, :])
                    d.drain().then_inc(s_ewTc, 1)
                    d.wait_ge(s_eet, 1)
                    d.tensor_copy(rhs_g[:, :, 0:D], bank[7][:, :].rearrange("p (a b) -> p a b", a=KD))
                    d.tensor_copy(rhs_g[:, :, D], nw)
                    d.drain().then_inc(s_eet, 1)
            staged(d, first)
            d.tensor_reduce(cs(0)[:, 0:1], logit[:, :], AX, ALU.max)
            d.drain().then_inc(s_red, 1)
            fast_dve(d)
            barrier(d)
            general_if(d, ga_dve)
            barrier(d)

            def second(st, nm, tr, pd):
                if tr:
                    front_hT(d, f1, *tr)
                if nm:
                    front_scale(d, f1, nm[0])
                if st:
                    front_stats(d, f1, x1[:, grp(st[0]), :], st[0])
                if tr:
                    g, k = tr
                    for b in range(GB):
                        d.tensor_tensor_reduce(out=sq[:, b, :], in0=hs[:, k, b, :], in1=hs[:, k, b, :], scale=1.0,
                                               scalar=0.0, op0=ALU.mult, op1=ALU.add,
                                               accum_out=S1g[:, k, b:b + 1])
                    d.drain()
                    d.tensor_copy(S1[:, grp(g)], S1g[:, k, :])
                    d.drain().then_inc(s_sq1, 1)
            staged(d, second)
            d.wait_ge(s_sq, 1)
            mobius_dve(d)
            d.drain().then_inc(s_gm, 1)
            d.wait_ge(s_ysz, 1)
            for g in range(1, NG, 2):
                for b in range(GB):
                    n = g * GB + b
                    d.tensor_scalar(ys[:, g, b, 0:D], mx[:, n, :], GR[:, n:n + 1], None, ALU.mult)
                d.tensor_copy(ys[:, g, :, D], GM1[:, g * GB:g * GB + GB])
                d.drain().then_inc(s_ys[1], 1)
            barrier(d)
            general_if(d, gm_dve, fm_dve)
            barrier(d)
            midpoint_dve(d)
            d.drain().then_inc(s_u, 1)
            for n in range(NB):
                d.wait_ge(s_us, n + 1)
                d.tensor_tensor(x1[:, n, :], nom[:, n, 0:D], x1[:, n, :], ALU.add).then_inc(s_o, 1)


_INS = ['x', 'adj', 'L0_gnn_weight', 'L0_gnn_bias', 'L0_gnn_node_w', 'L0_gnn_edge_w', 'L1_gnn_W']


def kernel(**inputs):
    import numpy as np
    import concourse.bacc as bacc
    from concourse.bass_utils import run_bass_kernel_spmd

    nc = bacc.Bacc("TRN2", target_bir_lowering=False, num_devices=1)
    arrays, args = {}, []
    for name in _INS:
        a = np.ascontiguousarray(inputs[name])
        arrays[f"in_{name}"] = a
        args.append(nc.dram_tensor(f"in_{name}", a.shape, mybir.dt.from_np(a.dtype), kind="ExternalInput").ap())
    out = nc.dram_tensor("out_0", inputs['x'].shape, F32, kind="ExternalOutput").ap()
    gnn_program(nc, *args, out)
    return run_bass_kernel_spmd(nc, [arrays], core_ids=[0]).results[0]["out_0"]
```
